# Optimizing a Trainium2 kernel written in Bass

```python
import numpy as np
import jax
import jax.numpy as jnp

def _softmax(x, axis=-1):
    return jax.nn.softmax(x, axis=axis)

def _gelu(x):
    return jax.nn.gelu(x, approximate=True)

def _silu(x):
    return jax.nn.silu(x)

def _sigmoid(x):
    return jax.nn.sigmoid(x)

def _layernorm(x, axis=-1, eps=1e-05):
    m = jnp.mean(x, axis=axis, keepdims=True)
    v = jnp.var(x, axis=axis, keepdims=True)
    return (x - m) / jnp.sqrt(v + eps)

def _scatter_add(tgt, idx, src, axis=0):
    return tgt.at[idx].add(src)

def _segment_sum(src, seg, n):
    return jax.ops.segment_sum(src, seg, n)
kernel_name = 'mk_seq_preln_d1_jaxref_r4_43890f'

def setup_inputs(seed: int=0):
    np.random.seed(seed)
    _w = jnp.asarray

    def _L0_attn_setup():
        import jax, jax.numpy as jnp
        import numpy as np
        HEADS = 32
        key = jax.random.key(seed)
        ks = jax.random.split(key, 5)
        H = 1024
        B, S = (2, 512)
        w_scale = 1.0 / np.sqrt(H)
        return {'x': jax.random.normal(ks[0], (B, S, H), dtype=jnp.float32), 'attn_qkvw': jax.random.normal(ks[1], (H, 3 * H), dtype=jnp.float32) * w_scale, 'attn_qkvb': jax.random.normal(ks[2], (3 * H,), dtype=jnp.float32) * 0.02, 'attn_ow': jax.random.normal(ks[3], (H, H), dtype=jnp.float32) * w_scale, 'attn_ob': jax.random.normal(ks[4], (H,), dtype=jnp.float32) * 0.02}
    _L0_attn_in = _L0_attn_setup()

    def _L0_ffn_setup():
        import jax, jax.numpy as jnp
        import numpy as np
        D = 1024
        F = 2752
        B, S = (4, 512)
        key = jax.random.key(seed)
        k_x, k_g, k_u, k_d = jax.random.split(key, 4)
        scale = 0.02
        return {'x': jax.random.normal(k_x, (B, S, D), dtype=jnp.float32), 'W_gate': jax.random.normal(k_g, (F, D), dtype=jnp.float32) * scale, 'W_up': jax.random.normal(k_u, (F, D), dtype=jnp.float32) * scale, 'W_down': jax.random.normal(k_d, (D, F), dtype=jnp.float32) * scale}
    _L0_ffn_in = _L0_ffn_setup()
    _d = {'L0_attn_x': _L0_attn_in['x'], 'L0_attn_attn_qkvw': _L0_attn_in['attn_qkvw'], 'L0_attn_attn_qkvb': _L0_attn_in['attn_qkvb'], 'L0_attn_attn_ow': _L0_attn_in['attn_ow'], 'L0_attn_attn_ob': _L0_attn_in['attn_ob'], 'L0_ffn_W_gate': _L0_ffn_in['W_gate'], 'L0_ffn_W_up': _L0_ffn_in['W_up'], 'L0_ffn_W_down': _L0_ffn_in['W_down']}
    _x0 = _d['L0_attn_x']
    _d['L0_attn_x'] = jax.random.normal(jax.random.fold_in(jax.random.key(seed), 1), (2, 1024, 1024), dtype=_x0.dtype)
    del _x0
    return _d

def reference(L0_attn_x, L0_attn_attn_qkvw, L0_attn_attn_qkvb, L0_attn_attn_ow, L0_attn_attn_ob, L0_ffn_W_gate, L0_ffn_W_up, L0_ffn_W_down):

    def _L0_attn_ref(x, attn_qkvw, attn_qkvb, attn_ow, attn_ob):
        import jax, jax.numpy as jnp
        import numpy as np
        HEADS = 32
        B, S, H = x.shape
        hd = H // HEADS
        scale = 1.0 / np.sqrt(hd)
        qkv = x @ attn_qkvw + attn_qkvb
        qkv = qkv.reshape(B, S, 3, HEADS, hd)
        q = jnp.transpose(qkv[:, :, 0], (0, 2, 1, 3))
        k = jnp.transpose(qkv[:, :, 1], (0, 2, 1, 3))
        v = jnp.transpose(qkv[:, :, 2], (0, 2, 1, 3))
        scores = jnp.einsum('bhqd,bhkd->bhqk', q, k) * scale
        probs = jax.nn.softmax(scores, axis=-1)
        ctx = jnp.einsum('bhqk,bhkd->bhqd', probs, v)
        ctx = jnp.transpose(ctx, (0, 2, 1, 3)).reshape(B, S, H)
        return ctx @ attn_ow + attn_ob

    def _L0_ffn_ref(x, W_gate, W_up, W_down):
        import jax, jax.numpy as jnp
        import numpy as np
        D = 1024
        F = 2752
        B, S = (4, 512)
        out_shape = x.shape[:-1] + (W_down.shape[0],)
        xt = x.reshape(-1, x.shape[-1])
        up = xt @ W_up.T
        gate = jax.nn.silu(xt @ W_gate.T)
        y = gate * up @ W_down.T
        return y.reshape(out_shape)
    x = L0_attn_x
    x = x + _L0_attn_ref(_layernorm(x, axis=-1), L0_attn_attn_qkvw, L0_attn_attn_qkvb, L0_attn_attn_ow, L0_attn_attn_ob)
    x = x + _L0_ffn_ref(_layernorm(x, axis=-1), L0_ffn_W_gate, L0_ffn_W_up, L0_ffn_W_down)
    return x

_drawn_inputs = setup_inputs


def setup_inputs(seed=0):
    import zlib

    import numpy as np

    out = dict(_drawn_inputs(seed))
    spreads = {}
    factors = {'L0_attn_attn_qkvb': 2.756, 'L0_attn_attn_ob': 2.815}
    for name, (base, spread) in spreads.items():
        noise = np.random.default_rng([zlib.crc32(name.encode()), seed]).standard_normal(out[name].shape)
        drawn = base * np.exp(spread * noise) if base else spread * noise
        out[name] = jnp.asarray(drawn.astype(out[name].dtype))
    for name, factor in factors.items():
        out[name] = (out[name] * factor).astype(out[name].dtype)
    return out
```

```python
import concourse.bass as bass
from concourse import mybir
from contextlib import ExitStack


B, S, H, HEADS, HD, F = 2, 1024, 1024, 32, 32, 2752
P = 128
KT = H // P
TT = S // P
NF = (F + P - 1) // P
FL = F - (NF - 1) * P
GH = 8
NG = HEADS // GH
VW = 66
NPU = 3
LAG = 2
AHEAD = 11
EPS = 1e-5
SCALE = HD ** -0.5


def program(nc, x, wqkv, bqk, bv, wo, bo, wg, wu, wd, ident, out):
    f32, f32r = mybir.dt.float32, mybir.dt.float32r
    ALU, ACT, AX = mybir.AluOpType, mybir.ActivationFunctionType, mybir.AxisListType

    queues = {"pe": [], "act": [], "dve": [], "pool": [], "sp": []}
    ctx = ExitStack()

    class Sem:
        def __init__(self, name):
            self.sem, self.n = ctx.enter_context(nc.semaphore(name)), 0

    sems = {}

    def sem(name):
        if name not in sems:
            sems[name] = Sem(name)
        return sems[name]

    def do(eng, fn, s=None, by=1):
        if s is None:
            queues[eng].append(fn)
            return None
        c = sem(s)
        queues[eng].append(lambda e: fn(e).then_inc(c.sem, by))
        c.n += by
        return (s, c.n)

    waited = {}

    def wait(eng, *values):
        for v in values:
            if v is None or waited.get((eng, v[0]), 0) >= v[1]:
                continue
            waited[eng, v[0]] = v[1]
            c, n = sems[v[0]].sem, v[1]
            queues[eng].append(lambda e, c=c, n=n: e.wait_ge(c, n))

    def dma(dst, src, s, eng="sp"):
        dst, src = (a.bitcast(f32) if a.dtype == f32r else a for a in (dst, src))
        return do(eng, lambda e: e.dma_start(dst, src), s, 16)

    def phase():
        for eng in queues:
            wait(eng, *[(k, c.n) for k, c in sems.items() if c.n])

    class Phase:
        def __init__(self):
            self.stack = ExitStack()

        def sb(self, name, shape, dt=f32):
            return self.stack.enter_context(nc.sbuf_tensor(name, shape, dt))

    with ctx:
        ps = [ctx.enter_context(nc.psum_tensor(f"ps{i}", [P, 512], f32)) for i in range(8)]
        keep = Phase()
        ctx.enter_context(keep.stack)
        idt = keep.sb("idt", [P, P])
        bqk_c = keep.sb("bqk_c", [P, 2 * KT])
        bv_b = keep.sb("bv_b", [P, H])
        bo_b = keep.sb("bo_b", [P, H])
        mv = keep.sb("mv", [P, TT, 2])
        st6 = keep.sb("st6", [P, TT, 12])
        rs = keep.sb("rs", [P, 5, TT])
        xh = keep.sb("xh", [P, KT, S], f32r)
        xl = keep.sb("xl", [P, KT, S], f32r)

        lnp = Phase()
        with lnp.stack:
            ln_x = lnp.sb("ln_x", [P, TT, H])
            ln_n = lnp.sb("ln_n", [P, 2, H])

        atp = Phase()
        with atp.stack:
            wh = atp.sb("wh", [P, 2, KT, 256], f32r)
            wl = atp.sb("wl", [P, 2, KT, 256], f32r)
            wraw = atp.sb("wraw", [P, KT, 256])
            qst = [atp.sb(f"qst{i}", [98, S], f32r) for i in range(3)]
            kst = [atp.sb(f"kst{i}", [98, S], f32r) for i in range(3)]
            stg = [atp.sb(f"stg{i}", [P, 2, 512], f32r) for i in range(2)]
            vt = [atp.sb(f"vt{i}", [P, TT, GH, VW], f32r) for i in range(2)]
            vtmp = atp.sb("vtmp", [P, 256])
            pu = [atp.sb(f"pu{i}", [P, 512]) for i in range(NPU)]
            ph = [atp.sb(f"ph{i}", [P, 512], f32r) for i in range(NPU)]
            pl = [atp.sb(f"pl{i}", [P, 512], f32r) for i in range(NPU)]
            uu = [atp.sb(f"uu{i}", [65, S]) for i in range(2)]
            mx = atp.sb("mx", [P, 2, TT, 2])
            mm = atp.sb("mm", [P, 2, TT])
            mh = atp.sb("mh", [TT, 2, P], f32r)
            ml = atp.sb("ml", [TT, 2, P], f32r)

        tail = Phase()
        with tail.stack:
            y = tail.sb("y", [P, TT, H])
            opp = Phase()
            with opp.stack:
                oraw = opp.sb("oraw", [P, KT, 256])
                oh = opp.sb("oh", [P, KT, H], f32r)
                ol = opp.sb("ol", [P, KT, H], f32r)
                ca = [opp.sb(f"ca{i}", [P, S]) for i in range(2)]
                cb = [opp.sb(f"cb{i}", [P, S]) for i in range(2)]
                cr = [opp.sb(f"cr{i}", [P, S]) for i in range(2)]
                zt = opp.sb("zt", [P, 256])
            l2p = Phase()
            with l2p.stack:
                l2_n = l2p.sb("l2_n", [P, 2, H])
            ffp = Phase()
            with ffp.stack:
                graw = [ffp.sb(f"graw{i}", [P, KT, P]) for i in range(2)]
                draw = ffp.sb("draw", [P, H])
                gh = [ffp.sb(f"gh{i}", [P, KT, P], f32r) for i in range(3)]
                gl = [ffp.sb(f"gl{i}", [P, KT, P], f32r) for i in range(3)]
                dh = [ffp.sb(f"dh{i}", [P, H], f32r) for i in range(3)]
                dl = [ffp.sb(f"dl{i}", [P, H], f32r) for i in range(3)]
                hh = [ffp.sb(f"hh{i}", [P, S], f32r) for i in range(4)]
                hl = [ffp.sb(f"hl{i}", [P, S], f32r) for i in range(4)]
                sg = [ffp.sb(f"sg{i}", [P, 512]) for i in range(2)]
                hf = [ffp.sb(f"hf{i}", [P, 512]) for i in range(2)]

        q_d = nc.dram_tensor("q_d", (B, HEADS, 96, S), f32, kind="Internal").ap()
        k_d = nc.dram_tensor("k_d", (B, HEADS, 96, S), f32, kind="Internal").ap()
        c_d = nc.dram_tensor("c_d", (B, 2, H, S), f32, kind="Internal").ap()
        z_d = nc.dram_tensor("z_d", (B, HEADS, S), f32, kind="Internal").ap()
        r_d = nc.dram_tensor("r_d", (B, HEADS, S), f32, kind="Internal").ap()

        dma(idt[:, :], ident, "d_const")
        dma(bqk_c[:, :], bqk, "d_const")
        dma(bv_b[:, :], bv.partition_broadcast(P), "d_const")
        const = dma(bo_b[:, :], bo.partition_broadcast(P), "d_const")

        def mm3(dst, ah, al, bh, bl, n, i, tag=None):
            for j, (l, r) in enumerate(((ah, bh), (al, bh), (ah, bl))):
                last = i == n - 1 and j == 2
                t = do("pe", lambda e, l=l, r=r, j=j, last=last: e.matmul(dst, l, r, start=(i == 0 and j == 0), stop=last),
                       tag if last else None)
            return t

        def layernorm(src, loaded, nbuf, bank0):
            for t in range(TT):
                wait("dve", loaded[t])
                for j in range(2):
                    a = do("dve", lambda e, t=t, j=j: e.bn_stats(st6[:, t, 6 * j:6 * j + 6], src[:, t, 512 * j:512 * j + 512]), "v_st")
            wait("dve", a)
            for t in range(TT):
                a = do("dve", lambda e, t=t: e.bn_aggr(mv[:, t, :], st6[:, t, :]), "v_st")
            wait("dve", a)
            v, s, r, u = rs[:, 0, :], rs[:, 1, :], rs[:, 2, :], rs[:, 3, :]
            a = do("dve", lambda e: e.tensor_scalar(v, mv[:, :, 1], EPS, None, ALU.add), "v_var")
            wait("act", a)
            b = do("act", lambda e: e.activation(s, v, ACT.Sqrt), "a_sd")
            wait("dve", b)
            c = do("dve", lambda e: e.reciprocal(r, s), "v_st")
            for k in range(1):
                wait("dve", c)
                c = do("dve", lambda e: e.tensor_tensor(u, r, r, ALU.mult), "v_st")
                wait("dve", c)
                c = do("dve", lambda e: e.tensor_tensor(u, u, v, ALU.mult), "v_st")
                wait("dve", c)
                c = do("dve", lambda e: e.tensor_scalar(u, u, -0.5, 1.5, ALU.mult, ALU.add), "v_st")
                wait("dve", c)
                c = do("dve", lambda e: e.tensor_tensor(rs[:, 4, :], r, u, ALU.mult), "v_st")
            wait("dve", c)
            tr = [None] * TT
            ev = [None] * (2 * TT)
            for t in range(TT):
                wait("dve", tr[t - 2] if t >= 2 else None)
                n = do("dve", lambda e, t=t: e.tensor_scalar(nbuf[:, t % 2, :], src[:, t, :], mv[:, t, 0:1], rs[:, 4, t:t + 1],
                                                             ALU.subtract, ALU.mult), "v_n")
                wait("pe", n, const)
                for g in range(2):
                    i = 2 * t + g
                    bk = ps[bank0 + i % 4]
                    wait("pe", ev[i - 4] if i >= 4 else None)
                    for k in range(4):
                        tr[t] = do("pe", lambda e, t=t, k=k, g=g, bk=bk: e.transpose(
                            bk[:, P * k:P * k + P], nbuf[:, t % 2, P * (4 * g + k):P * (4 * g + k) + P], idt[:, :]),
                            "p_tr" if k == 3 else None)
                    wait("act", tr[t])
                    pv = bk[:, :].rearrange("p (k c) -> p k c", k=4)
                    oh_, ol_ = (z[:, 4 * g:4 * g + 4, P * t:P * t + P] for z in (xh, xl))
                    a = do("act", lambda e, o=oh_, pv=pv: e.activation(o, pv, ACT.Copy), "a_xh")
                    wait("dve", a)
                    ev[i] = do("dve", lambda e, o=ol_, o2=oh_, pv=pv: e.tensor_tensor(o, pv, o2, ALU.subtract), "v_xl")
            return ev[-1]

        def attention(b):
            units = [(g, what) for g in range(NG) for what in (2, 0, 1)]
            w_ready, w_done = {}, {}
            raw_free = [None]

            def load_unit(i):
                g, what = units[i]
                slot = i % 2
                wait("sp", raw_free[0])
                d = dma(wraw[:, :, :], wqkv[what, g], "d_w")
                wait("pool", d, w_done.get(i - 2))
                a = do("pool", lambda e: e.tensor_scalar(wh[:, slot], wraw[:, :, :], 1.0, 0.0, ALU.mult, ALU.add), "g_wh")
                wait("dve", a, w_done.get(i - 2))
                raw_free[0] = w_ready[i] = do("dve", lambda e: e.tensor_tensor(wl[:, slot], wraw[:, :, :], wh[:, slot], ALU.subtract), "v_wl")

            nload = [0]

            def loaded(i):
                while nload[0] <= min(i, len(units) - 1):
                    load_unit(nload[0])
                    nload[0] += 1

            bank_free = [None]
            stg_free, nstg = [None, None], [0]
            qk_ready = {}
            v_ready = {}
            v_free = {}
            bgb = ps[6]

            def v_group(g):
                i = 3 * g
                loaded(i + 1)
                vv = vt[g % 2]
                wait("pe", w_ready[i])
                for t in range(TT):
                    wait("pe", bank_free[0])
                    for k in range(KT):
                        z = slice(P * t, P * t + P)
                        a = mm3(bgb[:, 0:256], xh[:, k, z], xl[:, k, z], wh[:, i % 2, k, :], wl[:, i % 2, k, :], KT, k, "p_v")
                        yield 1.5
                    wait("dve", a, v_free.get(g - 2))
                    wait("act", v_free.get(g - 2))
                    wait("dve", sem_last("v_vl"), sem_last("a_vh"))
                    c = do("dve", lambda e, g=g: e.tensor_tensor(vtmp[:, :], bgb[:, 0:256], bv_b[:, 256 * g:256 * g + 256], ALU.add), "v_v")
                    bank_free[0] = c
                    wait("act", c)
                    src = vtmp[:, :].rearrange("p (h d) -> p h d", d=HD)
                    hi, lo = vv[:, t, :, 0:HD], vv[:, t, :, HD:2 * HD]
                    c = do("act", lambda e, hi=hi, src=src: e.activation(hi, src, ACT.Copy), "a_vh")
                    wait("dve", c)
                    v_ready[g] = do("dve", lambda e, hi=hi, lo=lo, src=src: e.tensor_tensor(lo, src, hi, ALU.subtract), "v_vl")
                w_done[i] = a

            def sem_last(name):
                c = sems.get(name)
                return (name, c.n) if c and c.n else None

            def qk_chunk(c, what):
                i = 3 * (c // 2) + 1 + what
                loaded(i + (c % 2))
                wait("pe", w_ready[i])
                cols = slice(P * (c % 2), P * (c % 2) + P)
                for half in range(2):
                    z = slice(512 * half, 512 * half + 512)
                    wait("pe", bank_free[0])
                    for k in range(KT):
                        a = mm3(bgb[:, :], wh[:, i % 2, k, cols], wl[:, i % 2, k, cols], xh[:, k, z], xl[:, k, z], KT, k, "p_qk")
                        yield 3
                    sl = nstg[0] % 2
                    nstg[0] += 1
                    bias = bqk_c[:, KT * what + c:KT * what + c + 1]
                    wait("act", a, stg_free[sl], const)
                    d = do("act", lambda e, sl=sl, bias=bias: e.activation(stg[sl][:, 0, :], bgb[:, :], ACT.Identity, bias=bias), "a_qh")
                    wait("dve", d, stg_free[sl])
                    bank_free[0] = d = do("dve", lambda e, sl=sl, bias=bias: e.scalar_tensor_tensor(
                        stg[sl][:, 1, :], bgb[:, :], bias, stg[sl][:, 0, :], ALU.add, ALU.subtract), "v_ql")
                    wait("sp", d)
                    hs = slice(4 * c, 4 * c + 4)
                    dst, three = (q_d, (0, 0, 1)) if what == 0 else (k_d, (0, 1, 0))
                    for r, part in enumerate(three):
                        for h in range(4 * c, 4 * c + 4):
                            o = HD * (h - 4 * c)
                            d = dma(dst[b, h, HD * r:HD * r + HD, z], stg[sl][o:o + HD, part, :], f"d_stg{sl}")
                    stg_free[sl] = d
                    qk_ready.setdefault(c, []).append(d)
                if c % 2:
                    w_done[i] = a

            def background():
                for c in range(1, KT):
                    if c % 2 == 0:
                        yield from v_group(c // 2)
                    yield from qk_chunk(c, 0)
                    yield from qk_chunk(c, 1)

            st_done, stack_ready, m_ready = {}, {}, {}
            st_free, a_free, pv_free = [None] * 2, [None] * 2, [None] * 2
            p_free = [None] * NPU
            u_free = [None] * 2
            seen = {"a": 0, "st": 0}
            ones = []
            for i in range(3):
                ones.append(do("dve", lambda e, i=i: e.memset(kst[i][96:98, :].bitcast(f32), -1.0), "v_one"))
            for i in range(2):
                ones.append(do("dve", lambda e, i=i: e.memset(vt[i][:, :, :, 64:65].bitcast(f32), 1.0), "v_one"))

            def load_stack(j):
                if j >= HEADS:
                    return
                wait("sp", *qk_ready[j // 4], st_done.get(j - 3))
                dma(qst[j % 3][0:96, :], q_d[b, j], f"d_st{j % 3}")
                stack_ready[j] = dma(kst[j % 3][0:96, :], k_d[b, j], f"d_st{j % 3}")

            def scores(j, t, half):
                wait("pe", stack_ready[j])
                if True:
                    n = seen["a"] % 2
                    seen["a"] += 1
                    bk = ps[2 + n]
                    wait("pe", a_free[n])
                    a = do("pe", lambda e, half=half, bk=bk: e.matmul(
                        bk[:, :], qst[j % 3][0:96, P * t:P * t + P], kst[j % 3][0:96, 512 * half:512 * half + 512],
                        start=True, stop=True), "p_a")
                    wait("dve", a)
                    a_free[n] = do("dve", lambda e, half=half, bk=bk: e.reduce_max(mx[:, j % 2, t, half:half + 1], bk[:, :], AX.X), "v_mx")
                if t == TT - 1 and half == 1:
                    wait("dve", a_free[0], a_free[1])
                    a = do("dve", lambda e: e.reduce_max(mm[:, j % 2, :], mx[:, j % 2, :, :], AX.X), "v_mm")
                    wait("pe", a, bank7[0])
                    a = do("pe", lambda e: e.transpose(ps[7][0:TT, 0:P], mm[:, j % 2, :], idt[:, :]), "p_m")
                    wait("dve", a, m_ready.get(j - 2))
                    c = do("dve", lambda e: e.tensor_copy(mh[:, j % 2, :], ps[7][0:TT, 0:P]), "v_mh")
                    wait("dve", c)
                    c = do("dve", lambda e: e.tensor_tensor(ml[:, j % 2, :], ps[7][0:TT, 0:P], mh[:, j % 2, :], ALU.subtract), "v_ml")
                    bank7[0] = c
                    wait("sp", c)
                    dma(qst[j % 3][96:97, :], mh[:, j % 2, :], f"d_m{j % 2}")
                    m_ready[j] = dma(qst[j % 3][97:98, :], ml[:, j % 2, :], f"d_m{j % 2}")

            bank7 = [None]
            pend = []

            def probs(j, t, half):
                if t == 0:
                    wait("pe", m_ready[j], *ones)
                if True:
                    n = seen["st"]
                    seen["st"] += 1
                    bk, sl = ps[n % 2], n % NPU
                    wait("pe", st_free[n % 2])
                    a = do("pe", lambda e, half=half, bk=bk: e.matmul(
                        bk[:, :], kst[j % 3][:, P * t:P * t + P], qst[j % 3][:, 512 * half:512 * half + 512],
                        start=True, stop=True), "p_st")
                    st_done[j] = a
                    wait("act", a, p_free[sl])
                    e1 = do("act", lambda e, sl=sl, bk=bk: e.activation(pu[sl][:, :], bk[:, :], ACT.Exp, scale=SCALE), "a_p")
                    st_free[n % 2] = e2 = do("act", lambda e, sl=sl, bk=bk: e.activation(ph[sl][:, :], bk[:, :], ACT.Exp, scale=SCALE), "a_ph")
                    eng = "pool" if n % 16 in POOL_PL else "dve"
                    wait(eng, e2, p_free[sl])
                    d = do(eng, lambda e, sl=sl: e.tensor_tensor(pl[sl][:, :], pu[sl][:, :], ph[sl][:, :], ALU.subtract),
                           "g_pl" if eng == "pool" else "v_pl")
                    pend.append((j, t, half, sl, e2, d))

            def context(j, t, half, sl, ready_h, ready_l):
                g = j // GH
                bk = ps[4 + half]
                vv = vt[g % 2][:, t, j % GH, 0:65]
                if t == 0:
                    wait("pe", pv_free[half], v_ready[g])
                wait("pe", ready_h)
                do("pe", lambda e: e.matmul(bk[0:65, :], vv, ph[sl][:, :], start=(t == 0), stop=False))
                wait("pe", ready_l)
                a = do("pe", lambda e: e.matmul(bk[0:65, :], vv, pl[sl][:, :], start=False, stop=(t == TT - 1)), "p_pv")
                p_free[sl] = a
                if t == TT - 1:
                    if j % GH == GH - 1:
                        v_free[g] = a
                    n = j % 2
                    wait("act", a, u_free[n])
                    pv_free[half] = c = do("act", lambda e: e.activation(uu[n][:, 512 * half:512 * half + 512], bk[0:65, :], ACT.Copy), "a_u")
                    if half == 1:
                        wait("sp", c)
                        dma(c_d[b, 0, HD * j:HD * j + HD, :], uu[n][0:HD, :], f"d_u{n}")
                        dma(c_d[b, 1, HD * j:HD * j + HD, :], uu[n][HD:2 * HD, :], f"d_u{n}")
                        u_free[n] = dma(z_d[b, j:j + 1, :], uu[n][64:65, :], f"d_u{n}")

            def run(gen):
                for _ in gen:
                    pass

            loaded(0)
            run(v_group(0))
            run(qk_chunk(0, 0))
            run(qk_chunk(0, 1))
            load_stack(0)
            load_stack(1)
            marks = [(0, 0), (16, 96), (48, 288), (80, 384), (112, 576), (144, 672), (176, 864), (208, 960)]

            def target(s):
                for (s0, w0), (s1, w1) in zip(marks, marks[1:]):
                    if s <= s1:
                        return w0 + (w1 - w0) * (s - s0) / (s1 - s0)
                return 1e9

            bg, spent = background(), 0
            def fill(s):
                nonlocal spent
                while spent < target(s) + 4:
                    w = next(bg, None)
                    if w is None:
                        break
                    spent += w

            for i in range(2 * AHEAD):
                scores(i // 16, i // 2 % TT, i % 2)
            for u in range(2 * HEADS * TT):
                j, t, half = u // 16, u // 2 % TT, u % 2
                if u % 16 == 0:
                    load_stack(j + 2)
                probs(j, t, half)
                n = u + 2 * AHEAD
                if n < 2 * HEADS * TT:
                    scores(n // 16, n // 2 % TT, n % 2)
                if len(pend) > LAG:
                    context(*pend.pop(0))
                fill((u + 1) / 2)
            while pend:
                context(*pend.pop(0))

        def project(b):
            d = dma(zt[:, :], z_d[b].rearrange("h (a n) -> (h a) n", n=256), "d_z")
            wait("dve", d)
            c = do("dve", lambda e: e.reciprocal(zt[:, :], zt[:, :]), "v_r")
            wait("sp", c)
            rdone = dma(r_d[b].rearrange("h (a n) -> (h a) n", n=256), zt[:, :], "d_r")
            xd = [dma(y[:, t, :], x[b, P * t:P * t + P, :], f"d_x{t}") for t in range(TT)]
            free = [None, None]
            o_free = [None]
            cready, oready = {}, {}

            def half(n):
                wait("sp", o_free[0])
                a = dma(oraw[:, :, :], wo[n], "d_o")
                wait("pool", a)
                z = slice(256 * n, 256 * n + 256)
                a = do("pool", lambda e: e.tensor_scalar(oh[:, :, z], oraw[:, :, :], 1.0, 0.0, ALU.mult, ALU.add), "g_oh")
                wait("dve", a)
                o_free[0] = oready[n] = do("dve", lambda e: e.tensor_tensor(ol[:, :, z], oraw[:, :, :], oh[:, :, z], ALU.subtract), "v_ol")

            def normalised(c):
                n = c % 2
                wait("sp", free[n], rdone)
                z = slice(P * c, P * c + P)
                dma(ca[n][:, :], c_d[b, 0, z, :], f"d_c{n}")
                dma(cb[n][:, :], c_d[b, 1, z, :], f"d_c{n}")
                for i in range(4):
                    d = dma(cr[n][HD * i:HD * i + HD, :], r_d[b, 4 * c + i, :].partition_broadcast(HD), f"d_c{n}")
                wait("dve", d)
                a = do("dve", lambda e: e.tensor_tensor(ca[n][:, :], ca[n][:, :], cb[n][:, :], ALU.add), "v_c")
                wait("dve", a)
                a = do("dve", lambda e: e.tensor_tensor(ca[n][:, :], ca[n][:, :], cr[n][:, :], ALU.mult), "v_c")
                wait("act", a)
                a = do("act", lambda e: e.activation(xh[:, c, :], ca[n][:, :], ACT.Copy), "a_ch")
                wait("dve", a)
                free[n] = cready[c] = do("dve", lambda e: e.tensor_tensor(xl[:, c, :], ca[n][:, :], xh[:, c, :], ALU.subtract), "v_cl")
            half(0)
            for c in range(KT):
                normalised(c)
                if c in (1, 3, 5):
                    half((c + 1) // 2)
            ybo = []
            for t in range(TT):
                wait("pool", xd[t], const)
                ybo.append(do("pool", lambda e, t=t: e.tensor_tensor(y[:, t, :], y[:, t, :], bo_b[:, :], ALU.add), "g_y"))
            bfree = [None] * 4
            ydone = []
            i = 0
            for t in range(TT):
                for hf_ in range(2):
                    z = slice(512 * hf_, 512 * hf_ + 512)
                    bk = ps[i % 4]
                    wait("pe", bfree[i % 4], oready[2 * hf_], oready[2 * hf_ + 1])
                    for c in range(KT):
                        wait("pe", cready[c])
                        q = slice(P * t, P * t + P)
                        a = mm3(bk[:, :], xh[:, c, q], xl[:, c, q], oh[:, c, z], ol[:, c, z], KT, c, "p_o")
                    wait("dve", a, ybo[t])
                    bfree[i % 4] = a = do("dve", lambda e, t=t, z=z, bk=bk: e.tensor_tensor(y[:, t, z], bk[:, :], y[:, t, z], ALU.add), "v_y")
                    i += 1
                ydone.append(a)
            return ydone

        def ffn(b):
            width = [P] * (NF - 1) + [FL]
            graw_free, gready, gfree = [None] * 2, {}, {}
            draw_free, dready, dfree = [None], {}, {}

            def load_gu(i):
                if i >= 2 * NF:
                    return
                f, w = divmod(i, 2)[0], width[i // 2]
                src = (wg, wu)[i % 2]
                r, sl = graw[i % 2], i % 3
                wait("sp", graw_free[i % 2])
                a = dma(r[:, :, :], src[f], f"d_g{i % 2}")
                wait("act", a, gfree.get(i - 3))
                a = do("act", lambda e: e.activation(gh[sl][:, :, :], r[:, :, :], ACT.Copy), "a_gh")
                wait("dve", a, gfree.get(i - 3))
                graw_free[i % 2] = gready[i] = do("dve", lambda e: e.tensor_tensor(gl[sl][:, :, :], r[:, :, :], gh[sl][:, :, :], ALU.subtract), "v_gl")

            def load_d(f):
                if f >= NF:
                    return
                sl, w = f % 3, width[f]
                wait("sp", draw_free[0])
                a = dma(draw[0:w, :], wd[P * f:P * f + w, :], "d_d")
                wait("pool", a, dfree.get(f - 3))
                a = do("pool", lambda e: e.tensor_scalar(dh[sl][0:w, :], draw[0:w, :], 1.0, 0.0, ALU.mult, ALU.add), "g_dh")
                wait("pool", a)
                draw_free[0] = dready[f] = do("pool", lambda e: e.tensor_tensor(dl[sl][0:w, :], draw[0:w, :], dh[sl][0:w, :], ALU.subtract), "g_dl")

            gfree_b = [None] * 4
            hready, hfree = {}, {}
            sg_free, hf_free = [None] * 2, [None] * 2
            yfree, ny = [None] * 4, [0]
            last = {}

            def gate_up(f):
                w = width[f]
                for what in range(2):
                    i = 2 * f + what
                    wait("pe", gready[i])
                    for half in range(2):
                        z = slice(512 * half, 512 * half + 512)
                        bk = ps[2 * what + half]
                        wait("pe", gfree_b[2 * what + half])
                        for k in range(KT):
                            a = mm3(bk[0:w, :], gh[i % 3][:, k, 0:w], gl[i % 3][:, k, 0:w], xh[:, k, z], xl[:, k, z], KT, k, "p_g")
                        if what == 0:
                            wait("act", a, sg_free[half])
                            gfree_b[half] = sgd[half] = do("act", lambda e, half=half, bk=bk: e.activation(
                                sg[half][0:w, :], bk[0:w, :], ACT.Silu), "a_sg")
                        else:
                            wait("dve", a, sgd[half], hf_free[half])
                            gfree_b[2 + half] = sg_free[half] = c = do("dve", lambda e, half=half, bk=bk: e.tensor_tensor(
                                hf[half][0:w, :], bk[0:w, :], sg[half][0:w, :], ALU.mult), "v_h")
                            wait("act", c, hfree.get(f - 4))
                            c = do("act", lambda e, half=half, z=z: e.activation(hh[f % 4][0:w, z], hf[half][0:w, :], ACT.Copy), "a_hh")
                            wait("dve", c, hfree.get(f - 4))
                            hf_free[half] = c = do("dve", lambda e, half=half, z=z: e.tensor_tensor(
                                hl[f % 4][0:w, z], hf[half][0:w, :], hh[f % 4][0:w, z], ALU.subtract), "v_hl")
                            hready.setdefault(f, []).append(c)
                    gfree[i] = a

            def down(fs):
                for t in range(TT):
                    for half in range(2):
                        n = ny[0] % 4
                        ny[0] += 1
                        bk = ps[4 + n]
                        z = slice(512 * half, 512 * half + 512)
                        q = slice(P * t, P * t + P)
                        wait("pe", yfree[n])
                        for i, f in enumerate(fs):
                            w = width[f]
                            wait("pe", *hready[f], dready[f])
                            a = mm3(bk[:, :], hh[f % 4][0:w, q], hl[f % 4][0:w, q], dh[f % 3][0:w, z], dl[f % 3][0:w, z], len(fs), i, "p_y")
                        wait("dve", a, last.get((t, half)))
                        last[t, half] = yfree[n] = do("dve", lambda e, t=t, z=z, bk=bk: e.tensor_tensor(y[:, t, z], bk[:, :], y[:, t, z], ALU.add), "v_y")
                    if fs[-1] == NF - 1:
                        wait("sp", yfree[n], last[t, 0])
                        dma(out[b, P * t:P * t + P, :], y[:, t, :], "d_out")
                for f in fs:
                    hfree[f] = dfree[f] = a

            sgd = [None] * 2
            groups = [[f, f + 1] for f in range(0, NF, 2)]
            for i in range(3):
                load_gu(i)
            load_d(0)
            load_d(1)
            todo = []
            for f in range(NF):
                gate_up(f)
                load_gu(2 * f + 3)
                load_gu(2 * f + 4)
                if todo and f % 2 == 0:
                    fs = todo.pop(0)
                    down(fs)
                    load_d(fs[-1] + 1)
                    load_d(fs[-1] + 2)
                if f % 2 == 1:
                    todo.append(groups[f // 2])
            for fs in todo:
                down(fs)

        for b in range(B):
            loads = [dma(ln_x[:, t, :], x[b, P * t:P * t + P, :], f"d_x{t}") for t in range(TT)]
            layernorm(ln_x, loads, ln_n, 0)
            phase()
            attention(b)
            phase()
            ydone = project(b)
            phase()
            layernorm(y, ydone, l2_n, 0)
            phase()
            ffn(b)
            phase()

        block = ctx.enter_context(nc.Block())

        def play(name):
            def body(e):
                for fn in queues[name]:
                    fn(e)
            return body

        block.tensor(play("pe"))
        block.scalar(play("act"))
        block.vector(play("dve"))
        block.gpsimd(play("pool"))
        block.sync(play("sp"))


POOL_PL = (1, 4, 7, 10, 13)


def kernel(L0_attn_x, L0_attn_attn_qkvw, L0_attn_attn_qkvb, L0_attn_attn_ow, L0_attn_attn_ob,
           L0_ffn_W_gate, L0_ffn_W_up, L0_ffn_W_down):
    import numpy as np
    import concourse.bacc as bacc
    from concourse.bass_utils import run_bass_kernel_spmd

    c = np.ascontiguousarray
    qkvb = np.asarray(L0_attn_attn_qkvb)

    def rows_first(w):
        pad = np.zeros((NF * P, H), w.dtype)
        pad[:F] = w
        return c(pad.reshape(NF, P, KT, P).transpose(0, 3, 2, 1))

    arrays = {
        "x": c(np.asarray(L0_attn_x)),
        "wqkv": c(np.asarray(L0_attn_attn_qkvw).reshape(KT, P, 3, NG, 256).transpose(2, 3, 1, 0, 4)),
        "bqk": c(qkvb[:2 * H].reshape(2 * KT, P).T),
        "bv": c(qkvb[2 * H:]),
        "wo": c(np.asarray(L0_attn_attn_ow).reshape(KT, P, 4, 256).transpose(2, 1, 0, 3)),
        "bo": c(np.asarray(L0_attn_attn_ob)),
        "wg": rows_first(np.asarray(L0_ffn_W_gate)),
        "wu": rows_first(np.asarray(L0_ffn_W_up)),
        "wd": c(np.asarray(L0_ffn_W_down).T),
        "ident": np.eye(P, dtype=np.float32),
    }
    nc = bacc.Bacc("TRN2", target_bir_lowering=False, num_devices=1)
    args = [nc.dram_tensor(f"in_{n}", a.shape, mybir.dt.from_np(a.dtype), kind="ExternalInput").ap() for n, a in arrays.items()]
    args.append(nc.dram_tensor("out_0", (B, S, H), mybir.dt.float32, kind="ExternalOutput").ap())
    program(nc, *args)
    r = run_bass_kernel_spmd(nc, [{f"in_{n}": a for n, a in arrays.items()}], core_ids=[0])
    return r.results[0]["out_0"]
```

```python
import concourse.bass as bass
from concourse import mybir
from contextlib import ExitStack


B, S, H, HEADS, HD, F = 2, 1024, 1024, 32, 32, 2752
P = 128
KT = H // P
TT = S // P
NF = (F + P - 1) // P
FL = F - (NF - 1) * P
GH = 8
NG = HEADS // GH
VW = 66
NPU = 5
LAG = 3
AHEAD = 12
EPS = 1e-5
SCALE = HD ** -0.5


def program(nc, x, wqkv, bqk, bv, wo, bo, wg, wu, wd, ident, out):
    f32, f32r = mybir.dt.float32, mybir.dt.float32r
    ALU, ACT, AX = mybir.AluOpType, mybir.ActivationFunctionType, mybir.AxisListType

    queues = {"pe": [], "act": [], "dve": [], "pool": [], "sp": []}
    ctx = ExitStack()

    class Sem:
        def __init__(self, name):
            self.sem, self.n = ctx.enter_context(nc.semaphore(name)), 0

    sems = {}

    def sem(name):
        if name not in sems:
            sems[name] = Sem(name)
        return sems[name]

    def do(eng, fn, s=None, by=1):
        if s is None:
            queues[eng].append(fn)
            return None
        c = sem(s)
        queues[eng].append(lambda e: fn(e).then_inc(c.sem, by))
        c.n += by
        return (s, c.n)

    waited = {}

    def wait(eng, *values):
        for v in values:
            if v is None or waited.get((eng, v[0]), 0) >= v[1]:
                continue
            waited[eng, v[0]] = v[1]
            c, n = sems[v[0]].sem, v[1]
            queues[eng].append(lambda e, c=c, n=n: e.wait_ge(c, n))

    def dma(dst, src, s, eng="sp"):
        dst, src = (a.bitcast(f32) if a.dtype == f32r else a for a in (dst, src))
        return do(eng, lambda e: e.dma_start(dst, src), s, 16)

    def phase():
        for eng in queues:
            wait(eng, *[(k, c.n) for k, c in sems.items() if c.n])

    class Phase:
        def __init__(self):
            self.stack = ExitStack()

        def sb(self, name, shape, dt=f32):
            return self.stack.enter_context(nc.sbuf_tensor(name, shape, dt))

    with ctx:
        ps = [ctx.enter_context(nc.psum_tensor(f"ps{i}", [P, 512], f32)) for i in range(8)]
        keep = Phase()
        ctx.enter_context(keep.stack)
        idt = keep.sb("idt", [P, P])
        bqk_c = keep.sb("bqk_c", [P, 2 * KT])
        bv_b = keep.sb("bv_b", [P, H])
        mv = keep.sb("mv", [P, TT, 2])
        st6 = keep.sb("st6", [P, TT, 12])
        rs = keep.sb("rs", [P, 5, TT])
        xh = keep.sb("xh", [P, KT, S], f32r)
        xl = keep.sb("xl", [P, KT, S], f32r)

        lnp = Phase()
        with lnp.stack:
            ln_x = lnp.sb("ln_x", [P, TT, H])
            ln_n = lnp.sb("ln_n", [P, 2, H])

        atp = Phase()
        with atp.stack:
            wh = atp.sb("wh", [P, 2, KT, 256], f32r)
            wl = atp.sb("wl", [P, 2, KT, 256], f32r)
            wraw = atp.sb("wraw", [P, KT, 256])
            qst = [atp.sb(f"qst{i}", [98, S], f32r) for i in range(3)]
            kst = [atp.sb(f"kst{i}", [98, S], f32r) for i in range(3)]
            stg = [atp.sb(f"stg{i}", [P, 2, 512], f32r) for i in range(2)]
            vt = [atp.sb(f"vt{i}", [P, TT, GH, VW], f32r) for i in range(2)]
            vtmp = [atp.sb(f"vtmp{i}", [P, 256]) for i in range(2)]
            pu, pl = [], []
            for i in range(NPU):
                at = nc.sbuf_base
                pu.append(atp.sb(f"pu{i}", [P, 512]))
                assert nc.sbuf_base == at + 2048
                pl.append(nc.alloc_sbuf_tensor_at(f"pl{i}", [P, 512], f32r, offset=at))
            ph = [atp.sb(f"ph{i}", [P, 512], f32r) for i in range(NPU)]
            uu = [atp.sb(f"uu{i}", [65, S]) for i in range(2)]
            mx = atp.sb("mx", [P, 2, TT, 2])
            mm = atp.sb("mm", [P, 2, TT])
            mh = atp.sb("mh", [TT, 2, P], f32r)
            ml = atp.sb("ml", [TT, 2, P], f32r)

        tail = Phase()
        with tail.stack:
            y = tail.sb("y", [P, TT, H])
            opp = Phase()
            with opp.stack:
                oraw = opp.sb("oraw", [P, KT, 256])
                oh = opp.sb("oh", [P, KT, H], f32r)
                ol = opp.sb("ol", [P, KT, H], f32r)
                ca = [opp.sb(f"ca{i}", [P, S]) for i in range(2)]
                cb = [opp.sb(f"cb{i}", [P, S]) for i in range(2)]
                cr = [opp.sb(f"cr{i}", [P, S]) for i in range(2)]
                zt = opp.sb("zt", [P, 256])
                bo_b = opp.sb("bo_b", [P, H])
            l2p = Phase()
            with l2p.stack:
                l2_n = l2p.sb("l2_n", [P, 2, H])
            ffp = Phase()
            with ffp.stack:
                graw = [ffp.sb(f"graw{i}", [P, KT, P]) for i in range(2)]
                draw = ffp.sb("draw", [P, H])
                gh = [ffp.sb(f"gh{i}", [P, KT, P], f32r) for i in range(3)]
                gl = [ffp.sb(f"gl{i}", [P, KT, P], f32r) for i in range(3)]
                dh = [ffp.sb(f"dh{i}", [P, H], f32r) for i in range(3)]
                dl = [ffp.sb(f"dl{i}", [P, H], f32r) for i in range(3)]
                hh = [ffp.sb(f"hh{i}", [P, S], f32r) for i in range(4)]
                hl = [ffp.sb(f"hl{i}", [P, S], f32r) for i in range(4)]
                sg = [ffp.sb(f"sg{i}", [P, 512]) for i in range(2)]
                hf = [ffp.sb(f"hf{i}", [P, 512]) for i in range(2)]

        q_d = nc.dram_tensor("q_d", (B, HEADS, 96, S), f32, kind="Internal").ap()
        k_d = nc.dram_tensor("k_d", (B, HEADS, 96, S), f32, kind="Internal").ap()
        c_d = nc.dram_tensor("c_d", (B, 2, H, S), f32, kind="Internal").ap()
        z_d = nc.dram_tensor("z_d", (B, HEADS, S), f32, kind="Internal").ap()
        r_d = nc.dram_tensor("r_d", (B, HEADS, S), f32, kind="Internal").ap()

        dma(idt[:, :], ident, "d_const")
        dma(bqk_c[:, :], bqk, "d_const")
        const = dma(bv_b[:, :], bv.partition_broadcast(P), "d_const")

        def mm3(dst, ah, al, bh, bl, n, i, tag=None):
            for j, (l, r) in enumerate(((ah, bh), (al, bh), (ah, bl))):
                last = i == n - 1 and j == 2
                t = do("pe", lambda e, l=l, r=r, j=j, last=last: e.matmul(dst, l, r, start=(i == 0 and j == 0), stop=last),
                       tag if last else None)
            return t

        def layernorm(src, loaded, nbuf, bank0):
            for t in range(TT):
                wait("dve", loaded[t])
                for j in range(2):
                    a = do("dve", lambda e, t=t, j=j: e.bn_stats(st6[:, t, 6 * j:6 * j + 6], src[:, t, 512 * j:512 * j + 512]), "v_st")
            wait("dve", a)
            for t in range(TT):
                a = do("dve", lambda e, t=t: e.bn_aggr(mv[:, t, :], st6[:, t, :]), "v_st")
            wait("dve", a)
            v, s, r, u = rs[:, 0, :], rs[:, 1, :], rs[:, 2, :], rs[:, 3, :]
            a = do("dve", lambda e: e.tensor_scalar(v, mv[:, :, 1], EPS, None, ALU.add), "v_var")
            wait("act", a)
            b = do("act", lambda e: e.activation(s, v, ACT.Sqrt), "a_sd")
            wait("dve", b)
            c = do("dve", lambda e: e.reciprocal(r, s), "v_st")
            for k in range(1):
                wait("dve", c)
                c = do("dve", lambda e: e.tensor_tensor(u, r, r, ALU.mult), "v_st")
                wait("dve", c)
                c = do("dve", lambda e: e.tensor_tensor(u, u, v, ALU.mult), "v_st")
                wait("dve", c)
                c = do("dve", lambda e: e.tensor_scalar(u, u, -0.5, 1.5, ALU.mult, ALU.add), "v_st")
                wait("dve", c)
                c = do("dve", lambda e: e.tensor_tensor(rs[:, 4, :], r, u, ALU.mult), "v_st")
            wait("dve", c)
            tr = [None] * TT
            ev = [None] * (2 * TT)
            for t in range(TT):
                wait("dve", tr[t - 2] if t >= 2 else None)
                n = do("dve", lambda e, t=t: e.tensor_scalar(nbuf[:, t % 2, :], src[:, t, :], mv[:, t, 0:1], rs[:, 4, t:t + 1],
                                                             ALU.subtract, ALU.mult), "v_n")
                wait("pe", n, const)
                for g in range(2):
                    i = 2 * t + g
                    bk = ps[bank0 + i % 4]
                    wait("pe", ev[i - 4] if i >= 4 else None)
                    for k in range(4):
                        tr[t] = do("pe", lambda e, t=t, k=k, g=g, bk=bk: e.transpose(
                            bk[:, P * k:P * k + P], nbuf[:, t % 2, P * (4 * g + k):P * (4 * g + k) + P], idt[:, :]),
                            "p_tr" if k == 3 else None)
                    wait("act", tr[t])
                    pv = bk[:, :].rearrange("p (k c) -> p k c", k=4)
                    oh_, ol_ = (z[:, 4 * g:4 * g + 4, P * t:P * t + P] for z in (xh, xl))
                    a = do("act", lambda e, o=oh_, pv=pv: e.activation(o, pv, ACT.Copy), "a_xh")
                    wait("dve", a)
                    ev[i] = do("dve", lambda e, o=ol_, o2=oh_, pv=pv: e.tensor_tensor(o, pv, o2, ALU.subtract), "v_xl")
            return ev[-1]

        def attention(b):
            deferred = []

            def defer(units, fn):
                deferred.append([units, fn])

            def due():
                for d in deferred:
                    d[0] -= 1
                for d in [d for d in deferred if d[0] <= 0]:
                    deferred.remove(d)
                    d[1]()

            def settled(ready, key):
                while key not in ready:
                    due()
                return ready[key]

            units = [(g, what) for g in range(NG) for what in (2, 0, 1)]
            w_ready, w_done = {}, {}
            raw_free = [None]

            def load_unit(i):
                g, what = units[i]
                slot = i % 2
                if i:
                    settled(w_ready, i - 1)
                wait("sp", raw_free[0])
                d = dma(wraw[:, :, :], wqkv[what, g], "d_w")

                def part(n):
                    z = slice(2 * n, 2 * n + 2)
                    wait("pool", d, w_done.get(i - 2))
                    a = do("pool", lambda e: e.tensor_scalar(wh[:, slot, z], wraw[:, z, :], 1.0, 0.0, ALU.mult, ALU.add), "g_wh")

                    def low():
                        wait("dve", a, w_done.get(i - 2))
                        b = do("dve", lambda e: e.tensor_tensor(wl[:, slot, z], wraw[:, z, :], wh[:, slot, z], ALU.subtract), "v_wl")
                        if n == 3:
                            raw_free[0] = w_ready[i] = b

                    defer(2, low)

                for n in range(4):
                    defer(5 + n, lambda n=n: part(n))

            nload = [0]

            def loaded(i):
                while nload[0] <= min(i, len(units) - 1):
                    load_unit(nload[0])
                    nload[0] += 1

            bank_free, nbank = {0: None, 1: None}, [0]
            stg_free, nstg = [None, None], [0]
            qk_ready = {}
            v_ready = {}
            v_free = {}

            def bg_bank():
                n = nbank[0] % 2
                nbank[0] += 1
                return n, ps[6 + n]

            def v_group(g):
                i = 3 * g
                loaded(i + 1)
                vv = vt[g % 2]
                wait("pe", settled(w_ready, i))
                for t in range(TT):
                    nb, bgb = bg_bank()
                    wait("pe", settled(bank_free, nb))
                    for k in range(KT):
                        z = slice(P * t, P * t + P)
                        a = mm3(bgb[:, 0:256], xh[:, k, z], xl[:, k, z], wh[:, i % 2, k, :], wl[:, i % 2, k, :], KT, k, "p_v")
                        yield 1.5
                    evacuate_v(g, t, a, nb, bgb)
                w_done[i] = a
                loaded(i + 2)

            vtmp_free, nv = [None, None], [0]

            def evacuate_v(g, t, a, nb, bgb):
                n = nv[0] % 2
                nv[0] += 1
                src = vtmp[n][:, :].rearrange("p (h d) -> p h d", d=HD)
                hi, lo = vt[g % 2][:, t, :, 0:HD], vt[g % 2][:, t, :, HD:2 * HD]
                bank_free.pop(nb, None)

                def biased():
                    wait("dve", a, vtmp_free[n], const)
                    bank_free[nb] = c = do("dve", lambda e: e.tensor_tensor(
                        vtmp[n][:, :], bgb[:, 0:256], bv_b[:, 256 * g:256 * g + 256], ALU.add), "v_v")
                    defer(1, lambda: high(c))

                def high(c):
                    wait("act", c, v_free.get(g - 2))
                    c = do("act", lambda e: e.activation(hi, src, ACT.Copy), "a_vh")
                    defer(1, lambda: low(c))

                def low(c):
                    wait("dve", c, v_free.get(g - 2))
                    vtmp_free[n] = c = do("dve", lambda e: e.tensor_tensor(lo, src, hi, ALU.subtract), "v_vl")
                    if t == TT - 1:
                        v_ready[g] = c

                defer(1, biased)

            def qk_chunk(c, what):
                i = 3 * (c // 2) + 1 + what
                loaded(i)
                wait("pe", settled(w_ready, i))
                cols = slice(P * (c % 2), P * (c % 2) + P)
                for half in range(2):
                    z = slice(512 * half, 512 * half + 512)
                    nb, bgb = bg_bank()
                    wait("pe", settled(bank_free, nb))
                    for k in range(KT):
                        a = mm3(bgb[:, :], wh[:, i % 2, k, cols], wl[:, i % 2, k, cols], xh[:, k, z], xl[:, k, z], KT, k, "p_qk")
                        yield 3
                    evacuate_qk(c, what, half, a, nb, bgb)
                if c % 2:
                    w_done[i] = a
                    loaded(i + 2)

            def evacuate_qk(c, what, half, a, nb, bgb):
                z = slice(512 * half, 512 * half + 512)
                sl = nstg[0] % 2
                nstg[0] += 1
                bias = bqk_c[:, KT * what + c:KT * what + c + 1]
                bank_free.pop(nb, None)

                def high():
                    wait("act", a, stg_free[sl], const)
                    d = do("act", lambda e: e.activation(stg[sl][:, 0, :], bgb[:, :], ACT.Identity, bias=bias), "a_qh")
                    defer(1, lambda: low(d))

                def low(d):
                    wait("dve", d, stg_free[sl])
                    bank_free[nb] = d = do("dve", lambda e: e.scalar_tensor_tensor(
                        stg[sl][:, 1, :], bgb[:, :], bias, stg[sl][:, 0, :], ALU.add, ALU.subtract), "v_ql")
                    wait("sp", d)
                    dst, three = (q_d, (0, 0, 1)) if what == 0 else (k_d, (0, 1, 0))
                    for r, part in enumerate(three):
                        for h in range(4 * c, 4 * c + 4):
                            o = HD * (h - 4 * c)
                            d = dma(dst[b, h, HD * r:HD * r + HD, z], stg[sl][o:o + HD, part, :], f"d_stg{sl}")
                    stg_free[sl] = d
                    qk_ready.setdefault(c, []).append(d)

                defer(1, high)

            def background():
                for c in range(1, KT):
                    if c % 2 == 0:
                        yield from v_group(c // 2)
                    yield from qk_chunk(c, 0)
                    yield from qk_chunk(c, 1)

            st_done, stack_ready, m_ready = {}, {}, {}
            st_free, a_free, pv_free = [None] * 2, [None] * 2, [None] * 2
            p_free = [None] * NPU
            u_free = [None] * 2
            seen = {"a": 0, "st": 0}
            ones = []
            for i in range(3):
                ones.append(do("dve", lambda e, i=i: e.memset(kst[i][96:98, :].bitcast(f32), -1.0), "v_one"))
            for i in range(2):
                ones.append(do("dve", lambda e, i=i: e.memset(vt[i][:, :, :, 64:65].bitcast(f32), 1.0), "v_one"))

            def load_stack(j):
                if j >= HEADS:
                    return
                while len(qk_ready.get(j // 4, ())) < 4:
                    due()
                wait("sp", *qk_ready[j // 4], st_done.get(j - 3))
                dma(qst[j % 3][0:96, :], q_d[b, j], f"d_st{j % 3}")
                stack_ready[j] = dma(kst[j % 3][0:96, :], k_d[b, j], f"d_st{j % 3}")

            def scores(j, t, half):
                wait("pe", stack_ready[j])
                if True:
                    n = seen["a"] % 2
                    seen["a"] += 1
                    bk = ps[2 + n]
                    wait("pe", a_free[n])
                    a = do("pe", lambda e, half=half, bk=bk: e.matmul(
                        bk[:, :], qst[j % 3][0:96, P * t:P * t + P], kst[j % 3][0:96, 512 * half:512 * half + 512],
                        start=True, stop=True), "p_a")
                    wait("dve", a)
                    a_free[n] = do("dve", lambda e, half=half, bk=bk: e.reduce_max(mx[:, j % 2, t, half:half + 1], bk[:, :], AX.X), "v_mx")
                if t == TT - 1 and half == 1:
                    wait("dve", a_free[0], a_free[1])
                    a = do("dve", lambda e: e.reduce_max(mm[:, j % 2, :], mx[:, j % 2, :, :], AX.X), "v_mm")
                    defer(2, lambda: maximum_to_rows(j, a))

            def maximum_to_rows(j, a):
                n = seen["a"] % 2
                seen["a"] += 1
                bk = ps[2 + n]
                wait("pe", a, a_free[n])
                a = do("pe", lambda e: e.transpose(bk[0:TT, 0:P], mm[:, j % 2, :], idt[:, :]), "p_m")

                def split():
                    wait("dve", a, m_ready.get(j - 2))
                    c = do("dve", lambda e: e.tensor_copy(mh[:, j % 2, :], bk[0:TT, 0:P]), "v_mh")
                    wait("dve", c)
                    a_free[n] = c = do("dve", lambda e: e.tensor_tensor(ml[:, j % 2, :], bk[0:TT, 0:P], mh[:, j % 2, :], ALU.subtract), "v_ml")
                    wait("sp", c)
                    dma(qst[j % 3][96:97, :], mh[:, j % 2, :], f"d_m{j % 2}")
                    m_ready[j] = dma(qst[j % 3][97:98, :], ml[:, j % 2, :], f"d_m{j % 2}")

                defer(1, split)

            pend = []

            def probs(j, t, half):
                if t == 0:
                    wait("pe", settled(m_ready, j), *ones)
                if True:
                    n = seen["st"]
                    seen["st"] += 1
                    bk, sl = ps[n % 2], n % NPU
                    wait("pe", st_free[n % 2])
                    a = do("pe", lambda e, half=half, bk=bk: e.matmul(
                        bk[:, :], kst[j % 3][:, P * t:P * t + P], qst[j % 3][:, 512 * half:512 * half + 512],
                        start=True, stop=True), "p_st")
                    st_done[j] = a
                    wait("act", a, p_free[sl])
                    e1 = do("act", lambda e, sl=sl, bk=bk: e.activation(pu[sl][:, :], bk[:, :], ACT.Exp, scale=SCALE), "a_p")
                    st_free[n % 2] = e2 = do("act", lambda e, sl=sl, bk=bk: e.activation(ph[sl][:, :], bk[:, :], ACT.Exp, scale=SCALE), "a_ph")
                    rest.append((j, t, half, sl, n, e2))

            rest = []

            def remainder(j, t, half, sl, n, e2):
                if True:
                    eng = "pool" if n % 16 in POOL_PL else "dve"
                    wait(eng, e2, p_free[sl])
                    d = do(eng, lambda e, sl=sl: e.tensor_tensor(pl[sl][:, :], pu[sl][:, :], ph[sl][:, :], ALU.subtract),
                           "g_pl" if eng == "pool" else "v_pl")
                    pend.append((j, t, half, sl, e2, d))

            def context(j, t, half, sl, ready_h, ready_l):
                g = j // GH
                bk = ps[4 + half]
                vv = vt[g % 2][:, t, j % GH, 0:65]
                if t == 0:
                    wait("pe", pv_free[half], settled(v_ready, g))
                wait("pe", ready_h)
                do("pe", lambda e: e.matmul(bk[0:65, :], vv, ph[sl][:, :], start=(t == 0), stop=False))
                wait("pe", ready_l)
                a = do("pe", lambda e: e.matmul(bk[0:65, :], vv, pl[sl][:, :], start=False, stop=(t == TT - 1)), "p_pv")
                p_free[sl] = a
                if t == TT - 1:
                    if j % GH == GH - 1:
                        v_free[g] = a
                    n = j % 2

                    def evacuate():
                        wait("act", a, u_free[n])
                        pv_free[half] = c = do("act", lambda e: e.activation(
                            uu[n][:, 512 * half:512 * half + 512], bk[0:65, :], ACT.Copy), "a_u")
                        if half == 1:
                            wait("sp", c)
                            dma(c_d[b, 0, HD * j:HD * j + HD, :], uu[n][0:HD, :], f"d_u{n}")
                            dma(c_d[b, 1, HD * j:HD * j + HD, :], uu[n][HD:2 * HD, :], f"d_u{n}")
                            u_free[n] = dma(z_d[b, j:j + 1, :], uu[n][64:65, :], f"d_u{n}")

                    defer(1, evacuate)

            def run(gen):
                for _ in gen:
                    due()

            loaded(0)
            run(v_group(0))
            run(qk_chunk(0, 0))
            run(qk_chunk(0, 1))
            load_stack(0)
            load_stack(1)
            marks = [(0, 0), (16, 96), (48, 288), (80, 384), (112, 576), (144, 672), (176, 864), (208, 960)]

            def target(s):
                for (s0, w0), (s1, w1) in zip(marks, marks[1:]):
                    if s <= s1:
                        return w0 + (w1 - w0) * (s - s0) / (s1 - s0)
                return 1e9

            bg, spent = background(), 0
            def fill(s):
                nonlocal spent
                while spent < target(s) + 4:
                    w = next(bg, None)
                    if w is None:
                        break
                    spent += w

            for i in range(2 * AHEAD):
                scores(i // 16, i // 2 % TT, i % 2)
                due()
            for u in range(2 * HEADS * TT):
                j, t, half = u // 16, u // 2 % TT, u % 2
                if u % 16 == 0:
                    load_stack(j + 2)
                probs(j, t, half)
                if len(rest) > 1:
                    remainder(*rest.pop(0))
                n = u + 2 * AHEAD
                if n < 2 * HEADS * TT:
                    scores(n // 16, n // 2 % TT, n % 2)
                due()
                if len(pend) > LAG:
                    context(*pend.pop(0))
                fill((u + 1) / 2)
            while rest:
                remainder(*rest.pop(0))
            while pend:
                context(*pend.pop(0))
                due()
            while deferred:
                due()

        def project(b):
            d = dma(zt[:, :], z_d[b].rearrange("h (a n) -> (h a) n", n=256), "d_z")
            wait("dve", d)
            c = do("dve", lambda e: e.reciprocal(zt[:, :], zt[:, :]), "v_r")
            wait("sp", c)
            bod = dma(bo_b[:, :], bo.partition_broadcast(P), "d_bo")
            rdone = dma(r_d[b].rearrange("h (a n) -> (h a) n", n=256), zt[:, :], "d_r")
            xd = [dma(y[:, t, :], x[b, P * t:P * t + P, :], f"d_x{t}") for t in range(TT)]
            free = [None, None]
            o_free = [None]
            cready, oready = {}, {}

            def half(n):
                wait("sp", o_free[0])
                a = dma(oraw[:, :, :], wo[n], "d_o")
                wait("pool", a)
                z = slice(256 * n, 256 * n + 256)
                a = do("pool", lambda e: e.tensor_scalar(oh[:, :, z], oraw[:, :, :], 1.0, 0.0, ALU.mult, ALU.add), "g_oh")
                wait("dve", a)
                o_free[0] = oready[n] = do("dve", lambda e: e.tensor_tensor(ol[:, :, z], oraw[:, :, :], oh[:, :, z], ALU.subtract), "v_ol")

            def normalised(c):
                n = c % 2
                wait("sp", free[n], rdone)
                z = slice(P * c, P * c + P)
                dma(ca[n][:, :], c_d[b, 0, z, :], f"d_c{n}")
                dma(cb[n][:, :], c_d[b, 1, z, :], f"d_c{n}")
                for i in range(4):
                    d = dma(cr[n][HD * i:HD * i + HD, :], r_d[b, 4 * c + i, :].partition_broadcast(HD), f"d_c{n}")
                wait("dve", d)
                a = do("dve", lambda e: e.tensor_tensor(ca[n][:, :], ca[n][:, :], cb[n][:, :], ALU.add), "v_c")
                wait("dve", a)
                a = do("dve", lambda e: e.tensor_tensor(ca[n][:, :], ca[n][:, :], cr[n][:, :], ALU.mult), "v_c")
                wait("act", a)
                a = do("act", lambda e: e.activation(xh[:, c, :], ca[n][:, :], ACT.Copy), "a_ch")
                wait("dve", a)
                free[n] = cready[c] = do("dve", lambda e: e.tensor_tensor(xl[:, c, :], ca[n][:, :], xh[:, c, :], ALU.subtract), "v_cl")
            half(0)
            for c in range(KT):
                normalised(c)
                if c in (1, 3, 5):
                    half((c + 1) // 2)
            ybo = []
            for t in range(TT):
                wait("pool", xd[t], bod)
                ybo.append(do("pool", lambda e, t=t: e.tensor_tensor(y[:, t, :], y[:, t, :], bo_b[:, :], ALU.add), "g_y"))
            bfree = [None] * 4
            ydone = []
            i = 0
            for t in range(TT):
                for hf_ in range(2):
                    z = slice(512 * hf_, 512 * hf_ + 512)
                    bk = ps[i % 4]
                    wait("pe", bfree[i % 4], oready[2 * hf_], oready[2 * hf_ + 1])
                    for c in range(KT):
                        wait("pe", cready[c])
                        q = slice(P * t, P * t + P)
                        a = mm3(bk[:, :], xh[:, c, q], xl[:, c, q], oh[:, c, z], ol[:, c, z], KT, c, "p_o")
                    wait("dve", a, ybo[t])
                    bfree[i % 4] = a = do("dve", lambda e, t=t, z=z, bk=bk: e.tensor_tensor(y[:, t, z], bk[:, :], y[:, t, z], ALU.add), "v_y")
                    i += 1
                ydone.append(a)
            return ydone

        def ffn(b):
            width = [P] * (NF - 1) + [FL]
            graw_free, gready, gfree = [None] * 2, {}, {}
            draw_free, dready, dfree = [None], {}, {}

            def load_gu(i):
                if i >= 2 * NF:
                    return
                f, w = divmod(i, 2)[0], width[i // 2]
                src = (wg, wu)[i % 2]
                r, sl = graw[i % 2], i % 3
                wait("sp", graw_free[i % 2])
                a = dma(r[:, :, :], src[f], f"d_g{i % 2}")
                wait("act", a, gfree.get(i - 3))
                a = do("act", lambda e: e.activation(gh[sl][:, :, :], r[:, :, :], ACT.Copy), "a_gh")
                wait("dve", a, gfree.get(i - 3))
                graw_free[i % 2] = gready[i] = do("dve", lambda e: e.tensor_tensor(gl[sl][:, :, :], r[:, :, :], gh[sl][:, :, :], ALU.subtract), "v_gl")

            def load_d(f):
                if f >= NF:
                    return
                sl, w = f % 3, width[f]
                wait("sp", draw_free[0])
                a = dma(draw[0:w, :], wd[P * f:P * f + w, :], "d_d")
                wait("pool", a, dfree.get(f - 3))
                a = do("pool", lambda e: e.tensor_scalar(dh[sl][0:w, :], draw[0:w, :], 1.0, 0.0, ALU.mult, ALU.add), "g_dh")
                wait("pool", a)
                draw_free[0] = dready[f] = do("pool", lambda e: e.tensor_tensor(dl[sl][0:w, :], draw[0:w, :], dh[sl][0:w, :], ALU.subtract), "g_dl")

            gfree_b = [None] * 4
            hready, hfree = {}, {}
            sg_free, hf_free = [None] * 2, [None] * 2
            yfree, ny = [None] * 4, [0]
            last = {}

            def gate_up(f):
                w = width[f]
                for what in range(2):
                    i = 2 * f + what
                    wait("pe", gready[i])
                    for half in range(2):
                        z = slice(512 * half, 512 * half + 512)
                        bk = ps[2 * what + half]
                        wait("pe", gfree_b[2 * what + half])
                        for k in range(KT):
                            a = mm3(bk[0:w, :], gh[i % 3][:, k, 0:w], gl[i % 3][:, k, 0:w], xh[:, k, z], xl[:, k, z], KT, k, "p_g")
                        if what == 0:
                            wait("act", a, sg_free[half])
                            gfree_b[half] = sgd[half] = do("act", lambda e, half=half, bk=bk: e.activation(
                                sg[half][0:w, :], bk[0:w, :], ACT.Silu), "a_sg")
                        else:
                            wait("dve", a, sgd[half], hf_free[half])
                            gfree_b[2 + half] = sg_free[half] = c = do("dve", lambda e, half=half, bk=bk: e.tensor_tensor(
                                hf[half][0:w, :], bk[0:w, :], sg[half][0:w, :], ALU.mult), "v_h")
                            wait("act", c, hfree.get(f - 4))
                            c = do("act", lambda e, half=half, z=z: e.activation(hh[f % 4][0:w, z], hf[half][0:w, :], ACT.Copy), "a_hh")
                            wait("dve", c, hfree.get(f - 4))
                            hf_free[half] = c = do("dve", lambda e, half=half, z=z: e.tensor_tensor(
                                hl[f % 4][0:w, z], hf[half][0:w, :], hh[f % 4][0:w, z], ALU.subtract), "v_hl")
                            hready.setdefault(f, []).append(c)
                    gfree[i] = a

            def down(fs):
                for t in range(TT):
                    for half in range(2):
                        n = ny[0] % 4
                        ny[0] += 1
                        bk = ps[4 + n]
                        z = slice(512 * half, 512 * half + 512)
                        q = slice(P * t, P * t + P)
                        wait("pe", yfree[n])
                        for i, f in enumerate(fs):
                            w = width[f]
                            wait("pe", *hready[f], dready[f])
                            a = mm3(bk[:, :], hh[f % 4][0:w, q], hl[f % 4][0:w, q], dh[f % 3][0:w, z], dl[f % 3][0:w, z], len(fs), i, "p_y")
                        wait("dve", a, last.get((t, half)))
                        last[t, half] = yfree[n] = do("dve", lambda e, t=t, z=z, bk=bk: e.tensor_tensor(y[:, t, z], bk[:, :], y[:, t, z], ALU.add), "v_y")
                    if fs[-1] == NF - 1:
                        wait("sp", yfree[n], last[t, 0])
                        dma(out[b, P * t:P * t + P, :], y[:, t, :], "d_out")
                for f in fs:
                    hfree[f] = dfree[f] = a

            sgd = [None] * 2
            groups = [[f, f + 1] for f in range(0, NF, 2)]
            for i in range(3):
                load_gu(i)
            load_d(0)
            load_d(1)
            todo = []
            for f in range(NF):
                gate_up(f)
                load_gu(2 * f + 3)
                load_gu(2 * f + 4)
                if todo and f % 2 == 0:
                    fs = todo.pop(0)
                    down(fs)
                    load_d(fs[-1] + 1)
                    load_d(fs[-1] + 2)
                if f % 2 == 1:
                    todo.append(groups[f // 2])
            for fs in todo:
                down(fs)

        for b in range(B):
            loads = [dma(ln_x[:, t, :], x[b, P * t:P * t + P, :], f"d_x{t}") for t in range(TT)]
            layernorm(ln_x, loads, ln_n, 0)
            phase()
            attention(b)
            phase()
            ydone = project(b)
            phase()
            layernorm(y, ydone, l2_n, 0)
            phase()
            ffn(b)
            phase()

        block = ctx.enter_context(nc.Block())

        def play(name):
            def body(e):
                for fn in queues[name]:
                    fn(e)
            return body

        block.tensor(play("pe"))
        block.scalar(play("act"))
        block.vector(play("dve"))
        block.gpsimd(play("pool"))
        block.sync(play("sp"))


POOL_PL = (1, 4, 7, 10, 13)


def kernel(L0_attn_x, L0_attn_attn_qkvw, L0_attn_attn_qkvb, L0_attn_attn_ow, L0_attn_attn_ob,
           L0_ffn_W_gate, L0_ffn_W_up, L0_ffn_W_down):
    import numpy as np
    import concourse.bacc as bacc
    from concourse.bass_utils import run_bass_kernel_spmd

    c = np.ascontiguousarray
    qkvb = np.asarray(L0_attn_attn_qkvb)

    def rows_first(w):
        pad = np.zeros((NF * P, H), w.dtype)
        pad[:F] = w
        return c(pad.reshape(NF, P, KT, P).transpose(0, 3, 2, 1))

    arrays = {
        "x": c(np.asarray(L0_attn_x)),
        "wqkv": c(np.asarray(L0_attn_attn_qkvw).reshape(KT, P, 3, NG, 256).transpose(2, 3, 1, 0, 4)),
        "bqk": c(qkvb[:2 * H].reshape(2 * KT, P).T),
        "bv": c(qkvb[2 * H:]),
        "wo": c(np.asarray(L0_attn_attn_ow).reshape(KT, P, 4, 256).transpose(2, 1, 0, 3)),
        "bo": c(np.asarray(L0_attn_attn_ob)),
        "wg": rows_first(np.asarray(L0_ffn_W_gate)),
        "wu": rows_first(np.asarray(L0_ffn_W_up)),
        "wd": c(np.asarray(L0_ffn_W_down).T),
        "ident": np.eye(P, dtype=np.float32),
    }
    nc = bacc.Bacc("TRN2", target_bir_lowering=False, num_devices=1)
    args = [nc.dram_tensor(f"in_{n}", a.shape, mybir.dt.from_np(a.dtype), kind="ExternalInput").ap() for n, a in arrays.items()]
    args.append(nc.dram_tensor("out_0", (B, S, H), mybir.dt.float32, kind="ExternalOutput").ap())
    program(nc, *args)
    r = run_bass_kernel_spmd(nc, [{f"in_{n}": a for n, a in arrays.items()}], core_ids=[0])
    return r.results[0]["out_0"]
```

```python
import concourse.bass as bass
from concourse import mybir
from contextlib import ExitStack


B, S, H, HEADS, HD, F = 2, 1024, 1024, 32, 32, 2752
P = 128
KT = H // P
TT = S // P
NF = (F + P - 1) // P
FL = F - (NF - 1) * P
GH = 8
NG = HEADS // GH
VW = 66
NPU = 5
LAG = 3
DIVIDE = 420
LEAD = 48
PACE = 3
AHEAD = 11
EPS = 1e-5
SCALE = HD ** -0.5


def program(nc, x, wqkv, bqk, bv, wo, bo, wg, wu, wd, ident, out):
    f32, f32r = mybir.dt.float32, mybir.dt.float32r
    ALU, ACT, AX = mybir.AluOpType, mybir.ActivationFunctionType, mybir.AxisListType

    queues = {"pe": [], "act": [], "dve": [], "pool": [], "sp": []}
    ctx = ExitStack()

    class Sem:
        def __init__(self, name):
            self.sem, self.n = ctx.enter_context(nc.semaphore(name)), 0

    sems = {}

    def sem(name):
        if name not in sems:
            sems[name] = Sem(name)
        return sems[name]

    def do(eng, fn, s=None, by=1):
        if s is None:
            queues[eng].append(fn)
            return None
        c = sem(s)
        queues[eng].append(lambda e: fn(e).then_inc(c.sem, by))
        c.n += by
        return (s, c.n)

    waited = {}

    def wait(eng, *values):
        for v in values:
            if v is None or waited.get((eng, v[0]), 0) >= v[1]:
                continue
            waited[eng, v[0]] = v[1]
            c, n = sems[v[0]].sem, v[1]
            queues[eng].append(lambda e, c=c, n=n: e.wait_ge(c, n))

    def dma(dst, src, s, eng="sp"):
        dst, src = (a.bitcast(f32) if a.dtype == f32r else a for a in (dst, src))
        return do(eng, lambda e: e.dma_start(dst, src), s, 16)

    def last(*names):
        return [(k, sems[k].n) for k in names if k in sems and sems[k].n]

    class Phase:
        def __init__(self):
            self.stack = ExitStack()

        def sb(self, name, shape, dt=f32):
            return self.stack.enter_context(nc.sbuf_tensor(name, shape, dt))

    with ctx:
        ps = [ctx.enter_context(nc.psum_tensor(f"ps{i}", [P, 512], f32)) for i in range(8)]
        keep = Phase()
        ctx.enter_context(keep.stack)
        idt = keep.sb("idt", [P, P])
        bqk_c = keep.sb("bqk_c", [P, 2 * KT])
        bv_b = keep.sb("bv_b", [P, H])
        mv = keep.sb("mv", [P, TT, 2])
        st6 = keep.sb("st6", [P, TT, 12])
        rs = keep.sb("rs", [P, 5, TT])
        xh = keep.sb("xh", [P, KT, S], f32r)
        xl = keep.sb("xl", [P, KT, S], f32r)

        mx = keep.sb("mx", [P, 2, TT, 2])
        mm = keep.sb("mm", [P, 2, TT])
        zt = [keep.sb(f"zt{i}", [P, HD]) for i in range(2)]
        zone = -(-nc.sbuf_base // 32) * 32

        def at(name, kb, shape, dt=f32):
            return nc.alloc_sbuf_tensor_at(name, shape, dt, offset=zone + int(1024 * kb))

        wh = at("wh", 0, [P, 2, KT, 256], f32r)
        wl = at("wl", 16, [P, 2, KT, 256], f32r)
        wraw = at("wraw", 32, [P, KT, 256])
        stg = [at(f"stg{i}", 40 + 4 * i, [P, 2, 512], f32r) for i in range(2)]
        qst = [at(f"qst{i}", 48 + 8 * i, [98, S], f32r) for i in range(3)]
        kst = [at(f"kst{i}", 52 + 8 * i, [98, S], f32r) for i in range(3)]
        pu = [at(f"pu{i}", 72 + 4 * i, [P, 512]) for i in range(NPU)]
        pl = [at(f"pl{i}", 72 + 4 * i, [P, 512], f32r) for i in range(NPU)]
        ph = [at(f"ph{i}", 74 + 4 * i, [P, 512], f32r) for i in range(NPU)]
        uu = [at(f"uu{i}", 92 + 4 * i, [65, S]) for i in range(2)]
        vtmp = [at(f"vtmp{i}", 100 + i, [P, 256]) for i in range(2)]
        mh = at("mh", 102, [TT, 2, P], f32r)
        ml = at("ml", 103, [TT, 2, P], f32r)
        vt = [at(f"vt{i}", (104, 120.5)[i], [P, TT, GH, VW], f32r) for i in range(2)]
        ln_x = [at(f"ln_x{i}", 80 + 4 * i, [P, H]) for i in range(4)]
        ln_n = [at(f"ln_n{i}", (40, 44, 120, 124)[i], [P, H]) for i in range(4)]
        oh = [at(f"oh{i}", (0, 8, 80, 88)[i], [P, KT, 256], f32r) for i in range(4)]
        ol = [at(f"ol{i}", (16, 24, 96, 104)[i], [P, KT, 256], f32r) for i in range(4)]
        oraw = at("oraw", 32, [P, KT, 256])
        ca2, cb2, cr2 = ([at(f"{n}{i}", (40, 112)[i] + k, [P, 512]) for i in range(2)] for n, k in (("ca", 0), ("cb", 2), ("cr", 4)))
        y = at("y", 48, [P, TT, H])
        nn = [at(f"nn{i}", (112, 116, 120, 124, 128, 132, 32, 36)[i], [P, H]) for i in range(TT)]
        bo_b = at("bo_b", 132, [P, H])
        gh = [at(f"gh{i}", 8 * i, [P, KT, P], f32r) for i in range(3)]
        gl = [at(f"gl{i}", 8 * i + 4, [P, KT, P], f32r) for i in range(3)]
        graw = [at(f"graw{i}", 24 + 4 * i, [P, KT, P]) for i in range(2)]
        draw = at("draw", 32, [P, H])
        sg = [at(f"sg{i}", 40 + 2 * i, [P, 512]) for i in range(2)]
        hf = [at(f"hf{i}", 44 + 2 * i, [P, 512]) for i in range(2)]
        hh = [at(f"hh{i}", (96, 104, 80, 88)[i], [P, S], f32r) for i in range(4)]
        hl = [at(f"hl{i}", (100, 108, 84, 92)[i], [P, S], f32r) for i in range(4)]
        dh = [at(f"dh{i}", 112 + 8 * i, [P, H], f32r) for i in range(3)]
        dl = [at(f"dl{i}", 116 + 8 * i, [P, H], f32r) for i in range(3)]

        q_d = nc.dram_tensor("q_d", (B, HEADS, 96, S), f32, kind="Internal").ap()
        k_d = nc.dram_tensor("k_d", (B, HEADS, 96, S), f32, kind="Internal").ap()
        c_d = nc.dram_tensor("c_d", (B, 2, H, S), f32, kind="Internal").ap()
        z_d = nc.dram_tensor("z_d", (B, HEADS, S), f32, kind="Internal").ap()
        r_d = nc.dram_tensor("r_d", (B, HEADS, S), f32, kind="Internal").ap()

        dma(idt[:, :], ident, "d_const")
        dma(bqk_c[:, :], bqk, "d_const")
        const = dma(bv_b[:, :], bv.partition_broadcast(P), "d_const")

        def mm3(dst, ah, al, bh, bl, n, i, tag=None):
            for j, (l, r) in enumerate(((ah, bh), (al, bh), (ah, bl))):
                last = i == n - 1 and j == 2
                t = do("pe", lambda e, l=l, r=r, j=j, last=last: e.matmul(dst, l, r, start=(i == 0 and j == 0), stop=last),
                       tag if last else None)
            return t

        def normalise(tiles, src, dst, ready, free):
            a0, a1 = tiles[0], tiles[-1] + 1
            for t in tiles:
                wait("dve", *ready[t])
                for j in range(2):
                    a = do("dve", lambda e, t=t, j=j: e.bn_stats(st6[:, t, 6 * j:6 * j + 6], src(t)[:, 512 * j:512 * j + 512]), "v_st")
            wait("dve", a)
            for t in tiles:
                a = do("dve", lambda e, t=t: e.bn_aggr(mv[:, t, :], st6[:, t, :]), "v_st")
            wait("dve", a)
            v, s, r, u, q = (rs[:, i, a0:a1] for i in range(5))
            a = do("dve", lambda e: e.tensor_scalar(v, mv[:, a0:a1, 1], EPS, None, ALU.add), "v_var")
            wait("act", a)
            b = do("act", lambda e: e.activation(s, v, ACT.Sqrt), "a_sd")
            wait("dve", b)
            c = do("dve", lambda e: e.reciprocal(r, s), "v_st")
            wait("dve", c)
            c = do("dve", lambda e: e.tensor_tensor(u, r, r, ALU.mult), "v_st")
            wait("dve", c)
            c = do("dve", lambda e: e.tensor_tensor(u, u, v, ALU.mult), "v_st")
            wait("dve", c)
            c = do("dve", lambda e: e.tensor_scalar(u, u, -0.5, 1.5, ALU.mult, ALU.add), "v_st")
            wait("dve", c)
            c = do("dve", lambda e: e.tensor_tensor(q, r, u, ALU.mult), "v_st")
            wait("dve", c)
            done = {}
            for t in tiles:
                wait("dve", *free(t))
                done[t] = do("dve", lambda e, t=t: e.tensor_scalar(dst(t)[:, :], src(t), mv[:, t, 0:1], rs[:, 4, t:t + 1],
                                                                   ALU.subtract, ALU.mult), "v_n")
            return done

        def transposed(t, src, ready, bank_free, x_free, bank=0):
            for g in range(2):
                n = bank + 2 * (t % 2) + g
                bk = ps[n]
                wait("pe", ready, const, bank_free[n])
                for k in range(4):
                    a = do("pe", lambda e, k=k, g=g, bk=bk: e.transpose(
                        bk[:, P * k:P * k + P], src[:, P * (4 * g + k):P * (4 * g + k) + P], idt[:, :]), "p_tr" if k == 3 else None)
                wait("act", a, *x_free)
                pv = bk[:, :].rearrange("p (k c) -> p k c", k=4)
                oh_, ol_ = (z[:, 4 * g:4 * g + 4, P * t:P * t + P] for z in (xh, xl))
                c = do("act", lambda e, o=oh_, pv=pv: e.activation(o, pv, ACT.Copy), "a_xh")
                wait("dve", c, *x_free)
                bank_free[n] = c = do("dve", lambda e, o=ol_, o2=oh_, pv=pv: e.tensor_tensor(o, pv, o2, ALU.subtract), "v_xl")
            return a, c

        def first_norm(b):
            mem = last("p_y")
            loads, tr, nd = {}, {}, {}

            def load(t):
                wait("sp", *mem, nd.get(t - 4))
                loads[t] = dma(ln_x[t % 4][:, :], x[b, P * t:P * t + P, :], f"d_x{t}")

            for t in range(4):
                load(t)
            yield
            small = last("a_sg", "v_h", "a_hh", "v_hl")
            xfree = last("p_g")
            bank_free = {n: None for n in range(4)}

            def pair(t0):
                tiles = [t0, t0 + 1]
                nd.update(normalise(tiles, lambda t: ln_x[t % 4][:, :], lambda t: ln_n[t % 4], {t: [loads[t]] for t in tiles},
                                    lambda t: [tr.get(t - 4)] + small + mem))
                for t in tiles:
                    if t + 4 < TT:
                        load(t + 4)

            pair(0)
            pair(2)
            yield
            wait("pe", *small)
            for t in range(TT):
                if t % 2 == 0 and 2 <= t < TT - 2:
                    pair(t + 2)
                tr[t], c = transposed(t, ln_n[t % 4], nd[t], bank_free, xfree)
                yield c

        def attention(b, norm):
            deferred = []

            def defer(units, fn):
                deferred.append([units, fn])

            def due():
                for d in deferred:
                    d[0] -= 1
                for d in [d for d in deferred if d[0] <= 0]:
                    deferred.remove(d)
                    d[1]()

            def settled(ready, key):
                while key not in ready:
                    due()
                return ready[key]

            weights_free = last("p_g", "v_gl", "a_gh", "g_dl")
            units = [(g, what) for g in range(NG) for what in (2, 0, 1)]
            w_ready, w_done = {}, {}
            raw_free = [None]

            def load_unit(i):
                g, what = units[i]
                slot = i % 2
                if i:
                    settled(w_ready, i - 1)
                wait("sp", raw_free[0], *weights_free)
                d = dma(wraw[:, :, :], wqkv[what, g], "d_w")

                def part(n):
                    z = slice(2 * n, 2 * n + 2)
                    wait("pool", d, w_done.get(i - 2), *weights_free)
                    a = do("pool", lambda e: e.tensor_scalar(wh[:, slot, z], wraw[:, z, :], 1.0, 0.0, ALU.mult, ALU.add), "g_wh")

                    def low():
                        eng = "dve" if i or b == 0 else "pool"
                        wait(eng, a, w_done.get(i - 2))
                        d = do(eng, lambda e: e.tensor_tensor(wl[:, slot, z], wraw[:, z, :], wh[:, slot, z], ALU.subtract),
                               "v_wl" if eng == "dve" else "g_wl")
                        if n == 3:
                            raw_free[0] = w_ready[i] = d

                    defer(2, low)

                for n in range(4):
                    defer(5 + n, lambda n=n: part(n))

            nload = [0]

            def loaded(i):
                while nload[0] <= min(i, len(units) - 1):
                    load_unit(nload[0])
                    nload[0] += 1

            bank_free, nbank = {0: None, 1: None}, [0]
            stg_free, nstg = [None, None], [0]
            qk_ready = {}
            v_ready = {}
            v_free = {}

            def bg_bank():
                n = nbank[0] % 2
                nbank[0] += 1
                return n, ps[6 + n]

            def v_group(g):
                i = 3 * g
                loaded(i + 1)
                vv = vt[g % 2]
                wait("pe", settled(w_ready, i))
                for t in range(TT):
                    nb, bgb = bg_bank()
                    wait("pe", settled(bank_free, nb), x_ready.get(t))
                    for k in range(KT):
                        z = slice(P * t, P * t + P)
                        a = mm3(bgb[:, 0:256], xh[:, k, z], xl[:, k, z], wh[:, i % 2, k, :], wl[:, i % 2, k, :], KT, k, "p_v")
                        yield 1.5
                    evacuate_v(g, t, a, nb, bgb)
                w_done[i] = a
                loaded(i + 2)

            vtmp_free, nv = [None, None], [0]

            def evacuate_v(g, t, a, nb, bgb):
                n = nv[0] % 2
                nv[0] += 1
                src = vtmp[n][:, :].rearrange("p (h d) -> p h d", d=HD)
                hi, lo = vt[g % 2][:, t, :, 0:HD], vt[g % 2][:, t, :, HD:2 * HD]
                bank_free.pop(nb, None)

                def biased():
                    wait("dve", a, vtmp_free[n], const, *tail_free)
                    bank_free[nb] = c = do("dve", lambda e: e.tensor_tensor(
                        vtmp[n][:, :], bgb[:, 0:256], bv_b[:, 256 * g:256 * g + 256], ALU.add), "v_v")
                    defer(1, lambda: high(c))

                def high(c):
                    wait("act", c, v_free.get(g - 2), *tail_free)
                    c = do("act", lambda e: e.activation(hi, src, ACT.Copy), "a_vh")
                    defer(1, lambda: low(c))

                def low(c):
                    wait("dve", c, v_free.get(g - 2))
                    vtmp_free[n] = c = do("dve", lambda e: e.tensor_tensor(lo, src, hi, ALU.subtract), "v_vl")
                    if t == TT - 1:
                        v_ready[g] = c

                defer(1, biased)

            def qk_chunk(c, what):
                i = 3 * (c // 2) + 1 + what
                loaded(i)
                wait("pe", settled(w_ready, i))
                cols = slice(P * (c % 2), P * (c % 2) + P)
                for half in range(2):
                    z = slice(512 * half, 512 * half + 512)
                    nb, bgb = bg_bank()
                    wait("pe", settled(bank_free, nb))
                    for k in range(KT):
                        a = mm3(bgb[:, :], wh[:, i % 2, k, cols], wl[:, i % 2, k, cols], xh[:, k, z], xl[:, k, z], KT, k, "p_qk")
                        yield 3
                    evacuate_qk(c, what, half, a, nb, bgb)
                if c % 2:
                    w_done[i] = a
                    loaded(i + 2)

            def evacuate_qk(c, what, half, a, nb, bgb):
                z = slice(512 * half, 512 * half + 512)
                sl = nstg[0] % 2
                nstg[0] += 1
                bias = bqk_c[:, KT * what + c:KT * what + c + 1]
                bank_free.pop(nb, None)

                def high():
                    wait("act", a, stg_free[sl], const, *last("p_tr"))
                    d = do("act", lambda e: e.activation(stg[sl][:, 0, :], bgb[:, :], ACT.Identity, bias=bias), "a_qh")
                    defer(1, lambda: low(d))

                def low(d):
                    wait("dve", d, stg_free[sl])
                    bank_free[nb] = d = do("dve", lambda e: e.scalar_tensor_tensor(
                        stg[sl][:, 1, :], bgb[:, :], bias, stg[sl][:, 0, :], ALU.add, ALU.subtract), "v_ql")
                    wait("sp", d)
                    dst, three = (q_d, (0, 0, 1)) if what == 0 else (k_d, (0, 1, 0))
                    for r, part in enumerate(three):
                        for h in range(4 * c, 4 * c + 4):
                            o = HD * (h - 4 * c)
                            d = dma(dst[b, h, HD * r:HD * r + HD, z], stg[sl][o:o + HD, part, :], f"d_stg{sl}")
                    stg_free[sl] = d
                    qk_ready.setdefault(c, []).append(d)

                defer(1, high)

            def background():
                for c in range(1, KT):
                    if c % 2 == 0:
                        yield from v_group(c // 2)
                    yield from qk_chunk(c, 0)
                    yield from qk_chunk(c, 1)

            st_done, stack_ready, m_ready = {}, {}, {}
            st_free, a_free, pv_free = [None] * 2, [None] * 2, [None] * 2
            p_free = [None] * NPU
            u_free = [None] * 2
            seen = {"a": 0, "st": 0}
            ones = []

            def load_stack(j):
                if j >= HEADS:
                    return
                while len(qk_ready.get(j // 4, ())) < 4:
                    due()
                wait("sp", *qk_ready[j // 4], st_done.get(j - 3))
                dma(qst[j % 3][0:96, :], q_d[b, j], f"d_st{j % 3}")
                stack_ready[j] = dma(kst[j % 3][0:96, :], k_d[b, j], f"d_st{j % 3}")

            def scores(j, t, half):
                wait("pe", stack_ready[j])
                n = seen["a"] % 2
                seen["a"] += 1
                bk = ps[2 + n]
                wait("pe", a_free[n])
                a = do("pe", lambda e, half=half, bk=bk: e.matmul(
                    bk[:, :], qst[j % 3][0:96, P * t:P * t + P], kst[j % 3][0:96, 512 * half:512 * half + 512],
                    start=True, stop=True), "p_a")
                wait("dve", a)
                a_free[n] = do("dve", lambda e, half=half, bk=bk: e.reduce_max(mx[:, j % 2, t, half:half + 1], bk[:, :], AX.X), "v_mx")
                if t == TT - 1 and half == 1:
                    wait("dve", a_free[0], a_free[1])
                    a = do("dve", lambda e: e.reduce_max(mm[:, j % 2, :], mx[:, j % 2, :, :], AX.X), "v_mm")
                    defer(2, lambda: maximum_to_rows(j, a))

            def maximum_to_rows(j, a):
                n = seen["a"] % 2
                seen["a"] += 1
                bk = ps[2 + n]
                wait("pe", a, a_free[n])
                a = do("pe", lambda e: e.transpose(bk[0:TT, 0:P], mm[:, j % 2, :], idt[:, :]), "p_m")

                def split():
                    wait("dve", a, m_ready.get(j - 2))
                    c = do("dve", lambda e: e.tensor_copy(mh[:, j % 2, :], bk[0:TT, 0:P]), "v_mh")
                    wait("dve", c)
                    a_free[n] = c = do("dve", lambda e: e.tensor_tensor(ml[:, j % 2, :], bk[0:TT, 0:P], mh[:, j % 2, :], ALU.subtract), "v_ml")
                    wait("sp", c)
                    dma(qst[j % 3][96:97, :], mh[:, j % 2, :], f"d_m{j % 2}")
                    m_ready[j] = dma(qst[j % 3][97:98, :], ml[:, j % 2, :], f"d_m{j % 2}")

                split()

            pend = []

            def probs(j, t, half):
                if t == 0:
                    wait("pe", settled(m_ready, j), *ones)
                n = seen["st"]
                seen["st"] += 1
                bk, sl = ps[n % 2], n % NPU
                wait("pe", st_free[n % 2])
                a = do("pe", lambda e, half=half, bk=bk: e.matmul(
                    bk[:, :], kst[j % 3][:, P * t:P * t + P], qst[j % 3][:, 512 * half:512 * half + 512],
                    start=True, stop=True), "p_st")
                st_done[j] = a
                wait("act", a, p_free[sl])
                e1 = do("act", lambda e, sl=sl, bk=bk: e.activation(pu[sl][:, :], bk[:, :], ACT.Exp, scale=SCALE), "a_p")
                st_free[n % 2] = e2 = do("act", lambda e, sl=sl, bk=bk: e.activation(ph[sl][:, :], bk[:, :], ACT.Exp, scale=SCALE), "a_ph")
                rest.append((j, t, half, sl, n, e2))

            rest = []

            def remainder(j, t, half, sl, n, e2):
                eng = "pool" if n % 16 in POOL_PL else "dve"
                wait(eng, e2, p_free[sl])
                d = do(eng, lambda e, sl=sl: e.tensor_tensor(pl[sl][:, :], pu[sl][:, :], ph[sl][:, :], ALU.subtract),
                       "g_pl" if eng == "pool" else "v_pl")
                pend.append((j, t, half, sl, e2, d))

            def context(j, t, half, sl, ready_h, ready_l):
                g = j // GH
                bk = ps[4 + half]
                vv = vt[g % 2][:, t, j % GH, 0:65]
                if t == 0:
                    wait("pe", pv_free[half], settled(v_ready, g))
                wait("pe", ready_h)
                do("pe", lambda e: e.matmul(bk[0:65, :], vv, ph[sl][:, :], start=(t == 0), stop=False))
                wait("pe", ready_l)
                a = do("pe", lambda e: e.matmul(bk[0:65, :], vv, pl[sl][:, :], start=False, stop=(t == TT - 1)), "p_pv")
                p_free[sl] = a
                if t == TT - 1:
                    if j % GH == GH - 1:
                        v_free[g] = a
                    n = j % 2

                    def evacuate():
                        wait("act", a, u_free[n])
                        pv_free[half] = c = do("act", lambda e: e.activation(
                            uu[n][:, 512 * half:512 * half + 512], bk[0:65, :], ACT.Copy), "a_u")
                        if half == 1:
                            wait("sp", c)
                            dma(c_d[b, 0, HD * j:HD * j + HD, :], uu[n][0:HD, :], f"d_u{n}")
                            dma(c_d[b, 1, HD * j:HD * j + HD, :], uu[n][HD:2 * HD, :], f"d_u{n}")
                            u_free[n] = dma(z_d[b, j:j + 1, :], uu[n][64:65, :], f"d_u{n}")
                            if j % 4 == 3:
                                sums.append((j // 4, u_free[0], u_free[1]))

                    evacuate()

            sums, inverse_ready, c_ready = [], {}, {}
            zt_free, c_free = [None, None], [None, None]
            wo_free, wo_ready = [None], {}

            def inverse(c, *stored):
                n = c % 2
                flat = lambda d: d[b, 4 * c:4 * c + 4, :].rearrange("h (a n) -> (h a) n", n=HD)
                wait("sp", *stored, zt_free[n])
                d = dma(zt[n][:, :], flat(z_d), f"d_z{n}")

                def divide():
                    wait("dve", d)
                    a = do("dve", lambda e: e.reciprocal(zt[n][:, :], zt[n][:, :]), "v_r")
                    wait("sp", a)
                    zt_free[n] = inverse_ready[c] = dma(flat(r_d), zt[n][:, :], f"d_r{n}")

                defer(6, divide)

            def divided(c, half, eng, n=0):
                settled(inverse_ready, c)
                ca, cb, cr = ca2[n], cb2[n], cr2[n]
                z, q = slice(P * c, P * c + P), slice(512 * half, 512 * half + 512)
                wait("sp", c_free[n], inverse_ready[c], *last("d_stg0", "d_stg1", "d_u0", "d_u1"), v_free[NG - 2] if n else None)
                dma(ca[:, :], c_d[b, 0, z, q], f"d_c{n}")
                dma(cb[:, :], c_d[b, 1, z, q], f"d_c{n}")
                for i in range(4):
                    d = dma(cr[HD * i:HD * i + HD, :], r_d[b, 4 * c + i, q].partition_broadcast(HD), f"d_c{n}")
                taken = last("p_qk", "p_v")

                def work():
                    wait(eng, d)
                    a = do(eng, lambda e: e.tensor_tensor(ca[:, :], ca[:, :], cb[:, :], ALU.add), "g_c")
                    wait(eng, a)
                    a = do(eng, lambda e: e.tensor_tensor(ca[:, :], ca[:, :], cr[:, :], ALU.mult), "g_c")
                    defer(3, lambda: high(a))

                def high(a):
                    wait("act", a, *taken)
                    a = do("act", lambda e: e.activation(xh[:, c, q], ca[:, :], ACT.Copy), "a_ch")
                    defer(1, lambda: low(a))

                def low(a):
                    wait("dve", a, *taken)
                    c_free[n] = c_ready[c, half] = do("dve", lambda e: e.tensor_tensor(
                        xl[:, c, q], ca[:, :], xh[:, c, q], ALU.subtract), "v_cl")

                defer(5, work)

            def load_wo(i, eng, *free):
                wait("sp", wo_free[0], *free)
                d = dma(oraw[:, :, :], wo[i], "d_o")

                def part(n):
                    z = slice(2 * n, 2 * n + 2)
                    wait(eng, d, *free)
                    if eng == "pool":
                        a = do("pool", lambda e: e.tensor_scalar(oh[i][:, z], oraw[:, z, :], 1.0, 0.0, ALU.mult, ALU.add), "g_oh")
                    else:
                        a = do("act", lambda e: e.activation(oh[i][:, z], oraw[:, z, :], ACT.Copy), "a_oh")

                    def low():
                        wait("dve", a, *free)
                        o = do("dve", lambda e: e.tensor_tensor(ol[i][:, z], oraw[:, z, :], oh[i][:, z], ALU.subtract), "v_ol")
                        if n == 3:
                            wo_free[0] = wo_ready[i] = o

                    defer(2, low)

                for n in range(4):
                    defer(5 + n, lambda n=n: part(n))

            def run(gen):
                for _ in gen:
                    due()

            x_ready = {}
            loaded(0)
            while deferred:
                due()
            yield
            tail_free = last("p_y", "v_y")
            wait("pe", *tail_free)
            first_v = v_group(0)
            for t in range(TT):
                x_ready[t] = next(norm)
                for _ in range(KT if t else 0):
                    next(first_v, None)
                    due()
            run(first_v)
            wait("pe", *last("v_xl"))
            run(qk_chunk(0, 0))
            run(qk_chunk(0, 1))
            while len(qk_ready.get(0, ())) < 4:
                due()
            mem = last("d_out", "v_y", "p_y", "v_n", "p_tr")
            wait("dve", *mem)
            for i in range(3):
                ones.append(do("dve", lambda e, i=i: e.memset(kst[i][96:98, :].bitcast(f32), -1.0), "v_one"))
            for i in range(2):
                ones.append(do("dve", lambda e, i=i: e.memset(vt[i][:, :, :, 64:65].bitcast(f32), 1.0), "v_one"))
            wait("sp", *mem)
            wait("act", *mem)
            wait("pool", *mem)
            wait("pe", *last("v_xl"))
            load_stack(0)
            load_stack(1)
            marks = [(0, 96), (48, 288), (80, 384), (112, 576), (144, 672), (176, 864), (208, 960)]

            def target(s):
                for (s0, w0), (s1, w1) in zip(marks, marks[1:]):
                    if s <= s1:
                        return w0 + (w1 - w0) * (s - s0) / (s1 - s0)
                return 1e9

            bg, spent = background(), 0
            def fill(s):
                nonlocal spent
                while spent < target(s) + 4:
                    w = next(bg, None)
                    if w is None:
                        break
                    spent += w

            while spent < LEAD:
                spent += next(bg)
                due()
            for i in range(2 * AHEAD):
                scores(i // 16, i // 2 % TT, i % 2)
                due()
                while spent < LEAD + PACE * (i + 1):
                    spent += next(bg)
            for u in range(2 * HEADS * TT):
                j, t, half = u // 16, u // 2 % TT, u % 2
                if u % 16 == 0:
                    load_stack(j + 2)
                if sums and u % 4 == 2:
                    inverse(*sums.pop(0))
                if u >= DIVIDE and (u - DIVIDE) % 6 == 0 and (u - DIVIDE) // 6 < 14:
                    n = (u - DIVIDE) // 6
                    divided(n // 2, n % 2, "pool", n % 2)
                if u in (DIVIDE, DIVIDE + 30):
                    load_wo(int(u > DIVIDE), "pool", *last("p_qk", "p_v", "v_wl"))
                probs(j, t, half)
                if len(rest) > 1:
                    remainder(*rest.pop(0))
                n = u + 2 * AHEAD
                if n < 2 * HEADS * TT:
                    scores(n // 16, n // 2 % TT, n % 2)
                due()
                if len(pend) > LAG:
                    context(*pend.pop(0))
                fill((u + 1) / 2)
            while rest:
                remainder(*rest.pop(0))
            while pend:
                context(*pend.pop(0))
                due()
            while deferred:
                due()
            inverse(*sums.pop(0))
            for half in range(2):
                divided(KT - 1, half, "dve", half)
            for half in range(2):
                settled(c_ready, (KT - 1, half))
            yield c_ready, wo_ready, load_wo, settled

        def project(b, gone, c_ready, wo_ready, load_wo, settled):
            wait("sp", *gone)
            settled(wo_ready, 1)
            load_wo(2, "act", *gone)
            xd = [dma(y[:, t, :], x[b, P * t:P * t + P, :], f"d_x{t}") for t in range(TT)]
            bod = dma(bo_b[:, :], bo.partition_broadcast(P), "d_bo")
            settled(wo_ready, 2)
            load_wo(3, "act", *gone)
            settled(wo_ready, 3)
            ybo = []
            for t in range(TT):
                wait("pool", xd[t], bod)
                ybo.append(do("pool", lambda e, t=t: e.tensor_tensor(y[:, t, :], y[:, t, :], bo_b[:, :], ALU.add), "g_y"))
            bank_free = [None] * 8
            wait("pe", *last("a_ph", "a_p", "v_mx", "v_ml", "a_u", "v_v", "v_ql"))
            yd, nd, half_done, later = {}, {}, {}, []

            def finish(t, half, bk, a):
                wait("dve", a, ybo[t])
                z = slice(512 * half, 512 * half + 512)
                bank_free[t] = yd[t, half] = do("dve", lambda e: e.tensor_tensor(y[:, t, z], bk[:, :], y[:, t, z], ALU.add), "v_y")
                if half == 1 and t % 2 == 1:
                    tiles = [t - 1, t]
                    nd.update(normalise(tiles, lambda t: y[:, t, :], lambda t: nn[t],
                                        {t: [yd[t, 0], yd[t, 1]] for t in tiles}, lambda t: last("g_y", "v_ol")))

            for half in range(2):
                for ts in ((0, 1, 2, 3), (4, 5, 6, 7)):
                    for cs in (range(KT - 1), (KT - 1,)):
                        for t in ts:
                            bk = ps[t]
                            q = slice(P * t, P * t + P)
                            wait("pe", bank_free[t], wo_ready[2 * half], wo_ready[2 * half + 1])
                            for c in cs:
                                wait("pe", c_ready[c, t // 4])
                                for n in range(2):
                                    z = slice(256 * n, 256 * n + 256)
                                    for j, (l, r) in enumerate(((xh, oh), (xl, oh), (xh, ol))):
                                        end = c == KT - 1 and j == 2
                                        a = do("pe", lambda e, l=l, r=r, c=c, n=n, j=j, end=end, q=q, z=z, bk=bk, half=half: e.matmul(
                                            bk[:, z], l[:, c, q], r[2 * half + n][:, c, :], start=(c == 0 and j == 0 and n == 0),
                                            stop=end, skip_group_check=True), "p_o" if end and n == 1 else None)
                            if c == KT - 1:
                                if half == 1 and t >= 4:
                                    later.append((t, half, bk, a))
                                else:
                                    finish(t, half, bk, a)
                half_done[half] = a
            yield nd, half_done, bank_free
            for args in later:
                finish(*args)
            yield

        def ffn(b, nd, half_done, o_free, rest_of_y, before_last, then):
            rows = [slice(0, P)] * (NF - 1) + [slice(P - FL, P)]
            graw_free, gready, gfree = [None] * 2, {}, {}
            draw_free, dready, dfree = [None], {}, {}

            def load_gu(i):
                if i >= 2 * NF - 1:
                    return
                f = i // 2
                src = (wg, wu)[i % 2]
                r, sl = graw[i % 2], i % 3
                wait("sp", graw_free[i % 2], half_done[0])
                a = dma(r[:, :, :], src[f], f"d_g{i % 2}")
                wait("act", a, gfree.get(i - 3), half_done[0])
                a = do("act", lambda e: e.activation(gh[sl][:, :, :], r[:, :, :], ACT.Copy), "a_gh")
                wait("dve", a, gfree.get(i - 3))
                graw_free[i % 2] = gready[i] = do("dve", lambda e: e.tensor_tensor(gl[sl][:, :, :], r[:, :, :], gh[sl][:, :, :], ALU.subtract), "v_gl")

            def load_d(f):
                if f >= NF:
                    return
                sl, w = f % 3, rows[f]
                wait("sp", draw_free[0], *n_gone)
                a = dma(draw[w, :], wd[P * f:P * f + w.stop - w.start, :], "d_d")
                wait("pool", a, dfree.get(f - 3))
                a = do("pool", lambda e: e.tensor_scalar(dh[sl][w, :], draw[w, :], 1.0, 0.0, ALU.mult, ALU.add), "g_dh")
                wait("pool", a)
                draw_free[0] = dready[f] = do("pool", lambda e: e.tensor_tensor(dl[sl][w, :], draw[w, :], dh[sl][w, :], ALU.subtract), "g_dl")

            hready, hfree = {}, {}
            sg_free, hf_free = [None] * 2, [None] * 2
            ny = [0]
            ysum = {}

            def gate_up(f):
                whats = (0, 1) if f < NF - 1 else (0,)
                order = [(what, half) for what in whats for half in range(2)]
                if f == 0:
                    order.sort(key=lambda o: o[1])
                for n, (what, half) in enumerate(order):
                    if f == 0 and n % 2 == 0:
                        for t in range(4 * half, 4 * half + 4):
                            x_ready.append(transposed(t, nn[t], nd[t], bank_free, [half_done[1]], 4 * half)[1])
                        wait("pe", *x_ready[4 * half:])
                        if half == 0:
                            gfree_b.extend(bank_free[n] for n in range(4))
                            rest_of_y()
                            bank_free.update((n, o_free[n]) for n in range(4, 8))
                        else:
                            yfree.extend(bank_free[4 + n] for n in range(4))
                            n_gone.extend(last("p_tr"))
                    product(f, what, half)

            def product(f, what, half):
                w, joined, i = rows[f], f == NF - 1, 2 * f + what
                z = slice(512 * half, 512 * half + 512)
                bk = ps[2 * what + half]
                wait("pe", gready[i], gfree_b[2 * what + half])
                for k in range(KT):
                    a = mm3(bk[:, :], gh[i % 3][:, k, :], gl[i % 3][:, k, :], xh[:, k, z], xl[:, k, z], KT, k, "p_g")
                gfree[i] = a
                if what == 0:
                    v = slice(0, w.stop - w.start)
                    wait("act", a, sg_free[half])
                    gfree_b[half] = sgd[half] = do("act", lambda e: e.activation(sg[half][w, :], bk[v, :], ACT.Silu), "a_sg")
                if what == 1 or joined:
                    wait("dve", a, sgd[half], hf_free[half])
                    gfree_b[2 * what + half] = sg_free[half] = c = do("dve", lambda e: e.tensor_tensor(
                        hf[half][w, :], bk[w, :], sg[half][w, :], ALU.mult), "v_h")
                    wait("act", c, hfree.get(f - 4))
                    c = do("act", lambda e: e.activation(hh[f % 4][w, z], hf[half][w, :], ACT.Copy), "a_hh")
                    wait("dve", c, hfree.get(f - 4))
                    hf_free[half] = c = do("dve", lambda e: e.tensor_tensor(hl[f % 4][w, z], hf[half][w, :], hh[f % 4][w, z], ALU.subtract), "v_hl")
                    hready.setdefault(f, []).append(c)

            def down(fs):
                for t in range(TT):
                    for half in range(2):
                        n = ny[0] % 4
                        ny[0] += 1
                        bk = ps[4 + n]
                        z = slice(512 * half, 512 * half + 512)
                        q = slice(P * t, P * t + P)
                        wait("pe", yfree[n])
                        for i, f in enumerate(fs):
                            w = rows[f]
                            wait("pe", *hready[f], dready[f])
                            a = mm3(bk[:, :], hh[f % 4][w, q], hl[f % 4][w, q], dh[f % 3][w, z], dl[f % 3][w, z], len(fs), i, "p_y")
                        wait("dve", a, ysum.get((t, half)))
                        ysum[t, half] = yfree[n] = do("dve", lambda e, t=t, z=z, bk=bk: e.tensor_tensor(y[:, t, z], bk[:, :], y[:, t, z], ALU.add), "v_y")
                    if fs[-1] == NF - 1:
                        wait("sp", yfree[n], ysum[t, 0])
                        dma(out[b, P * t:P * t + P, :], y[:, t, :], "d_out")
                for f in fs:
                    hfree[f] = dfree[f] = a

            sgd = [None] * 2
            groups = [[f, f + 1] for f in range(0, NF, 2)]
            load_gu(0)
            load_gu(1)
            bank_free = dict(enumerate(o_free))
            x_ready, gfree_b, yfree, n_gone = [], [], [], []
            todo = []
            for f in range(NF):
                gate_up(f)
                if f == 0:
                    load_gu(2)
                    load_d(0)
                    load_d(1)
                if f == NF - 1:
                    then()
                    before_last()
                load_gu(2 * f + 3)
                load_gu(2 * f + 4)
                if todo and f % 2 == 0:
                    fs = todo.pop(0)
                    down(fs)
                    if f == NF - 2:
                        before_last()
                    load_d(fs[-1] + 1)
                    load_d(fs[-1] + 2)
                if f % 2 == 1:
                    todo.append(groups[f // 2])
            for fs in todo:
                down(fs)

        norm = first_norm(0)
        next(norm)
        next(norm)
        heads = attention(0, norm)
        next(heads)
        for b in range(B):
            got = next(heads)
            gone = last("p_pv", "p_st", "p_a", "p_m", "a_u", "a_p", "a_ph", "v_pl", "g_pl", "v_mx", "v_mm", "v_ml", "d_m0", "d_m1", "d_u0", "d_u1",
                        "v_vl", "d_st0", "d_st1", "d_st2")
            rows = project(b, gone, *got)
            nd, half_done, o_free = next(rows)
            norm = first_norm(b + 1) if b + 1 < B else iter(())
            heads = attention(b + 1, norm) if b + 1 < B else iter(())
            ffn(b, nd, half_done, o_free, lambda: next(rows), lambda: next(norm, None), lambda: next(heads, None))
        wait("sp", *last(*sems))

        block = ctx.enter_context(nc.Block())

        def play(name):
            def body(e):
                for fn in queues[name]:
                    fn(e)
            return body

        block.tensor(play("pe"))
        block.scalar(play("act"))
        block.vector(play("dve"))
        block.gpsimd(play("pool"))
        block.sync(play("sp"))


POOL_PL = (1, 4, 7, 10, 13)


def kernel(L0_attn_x, L0_attn_attn_qkvw, L0_attn_attn_qkvb, L0_attn_attn_ow, L0_attn_attn_ob,
           L0_ffn_W_gate, L0_ffn_W_up, L0_ffn_W_down):
    import numpy as np
    import concourse.bacc as bacc
    from concourse.bass_utils import run_bass_kernel_spmd

    c = np.ascontiguousarray
    qkvb = np.asarray(L0_attn_attn_qkvb)

    w_gate, w_up = np.asarray(L0_ffn_W_gate), np.asarray(L0_ffn_W_up)

    def rows_first(w):
        return c(w.reshape(-1, P, KT, P).transpose(0, 3, 2, 1))

    arrays = {
        "x": c(np.asarray(L0_attn_x)),
        "wqkv": c(np.asarray(L0_attn_attn_qkvw).reshape(KT, P, 3, NG, 256).transpose(2, 3, 1, 0, 4)),
        "bqk": c(qkvb[:2 * H].reshape(2 * KT, P).T),
        "bv": c(qkvb[2 * H:]),
        "wo": c(np.asarray(L0_attn_attn_ow).reshape(KT, P, 4, 256).transpose(2, 1, 0, 3)),
        "bo": c(np.asarray(L0_attn_attn_ob)),
        "wg": rows_first(np.concatenate([w_gate, w_up[-FL:]])),
        "wu": rows_first(w_up[:F - FL]),
        "wd": c(np.asarray(L0_ffn_W_down).T),
        "ident": np.eye(P, dtype=np.float32),
    }
    nc = bacc.Bacc("TRN2", target_bir_lowering=False, num_devices=1)
    args = [nc.dram_tensor(f"in_{n}", a.shape, mybir.dt.from_np(a.dtype), kind="ExternalInput").ap() for n, a in arrays.items()]
    args.append(nc.dram_tensor("out_0", (B, S, H), mybir.dt.float32, kind="ExternalOutput").ap())
    program(nc, *args)
    r = run_bass_kernel_spmd(nc, [{f"in_{n}": a for n, a in arrays.items()}], core_ids=[0])
    return r.results[0]["out_0"]
```
